# Optimizing a Trainium2 kernel written in Bass

```python
import numpy as np
import jax
import jax.numpy as jnp

def _softmax(x, axis=-1):
    return jax.nn.softmax(x, axis=axis)

def _gelu(x):
    return jax.nn.gelu(x, approximate=True)

def _silu(x):
    return jax.nn.silu(x)

def _sigmoid(x):
    return jax.nn.sigmoid(x)

def _layernorm(x, axis=-1, eps=1e-05):
    m = jnp.mean(x, axis=axis, keepdims=True)
    v = jnp.var(x, axis=axis, keepdims=True)
    return (x - m) / jnp.sqrt(v + eps)

def _scatter_add(tgt, idx, src, axis=0):
    return tgt.at[idx].add(src)

def _segment_sum(src, seg, n):
    return jax.ops.segment_sum(src, seg, n)
kernel_name = 'mk_cond_resid_d4_seqx_r8_194fab'

def setup_inputs(seed: int=0):
    np.random.seed(seed)
    _w = jnp.asarray

    def _rec_inputs():
        import jax
        import jax.numpy as jnp
        _rk = jax.random.key(seed)
        x = -7.109e-05 + 0.9999 * jax.random.normal(jax.random.fold_in(_rk, 1), (8, 128, 512), jnp.float32)
        _lenS = 128 - jax.random.randint(jax.random.fold_in(_rk, 7), (8,), 0, max(1, 128 // 4) + 1, jnp.int32)
        _lenS2 = 128 - jax.random.randint(jax.random.fold_in(_rk, 8), (8,), 0, max(1, 128 // 4) + 1, jnp.int32)
        itok_B_0_15 = jax.random.randint(jax.random.fold_in(_rk, 11), (8,), 0, 16, jnp.int32)
        condB_coeff = 0.00219231 + 0.0100837 * jax.random.normal(jax.random.fold_in(_rk, 12), (8,), jnp.float32)
        itok_B_3_7 = jax.random.randint(jax.random.fold_in(_rk, 14), (8,), 3, 8, jnp.int32)
        itok_B_0_2 = jax.random.randint(jax.random.fold_in(_rk, 15), (8,), 0, 3, jnp.int32)
        _validS = jnp.arange(128)[None, :] < _lenS[:, None]
        _validS2 = jnp.arange(128)[None, :] < _lenS2[:, None]
        _causal = jnp.tril(jnp.ones((128, 128), dtype=bool))
        mask_Bx4096x4096_ik1 = jnp.where(jnp.ones((8, 512, 512), dtype=bool), 1, 0).astype(jnp.int32)
        return (x, itok_B_0_15, condB_coeff, itok_B_3_7, itok_B_0_2, mask_Bx4096x4096_ik1)
    x, itok_B_0_15, condB_coeff, itok_B_3_7, itok_B_0_2, mask_Bx4096x4096_ik1 = _rec_inputs()

    def _L0_cond_setup():
        import jax, jax.numpy as jnp
        import numpy as np
        SCALING = 16.0 / 16
        key = jax.random.key(seed)
        k1, k2, k3, k4, k5 = jax.random.split(key, 5)
        B, S, D_IN, D_OUT, R, N_ADPT = (8, 256, 512, 512, 16, 16)
        x = jax.random.normal(k1, (B, S, D_IN), dtype=jnp.float32)
        adapter_indices = jax.random.randint(k2, (B,), 0, N_ADPT, dtype=jnp.int32)
        W = jax.random.normal(k3, (D_IN, D_OUT), dtype=jnp.float32) * 0.02
        lora_A = jax.random.normal(k4, (N_ADPT, D_IN, R), dtype=jnp.float32) * 0.02
        lora_B = jax.random.normal(k5, (N_ADPT, R, D_OUT), dtype=jnp.float32) * 0.02
        return {'x': x, 'adapter_indices': adapter_indices, 'W': W, 'lora_A': lora_A, 'lora_B': lora_B}
    _L0_cond_all = _L0_cond_setup()
    _L0_cond_in = {k: v for k, v in _L0_cond_all.items() if k in ('W', 'lora_A', 'lora_B')}
    del _L0_cond_all

    def _L1_cond_setup():
        import jax, jax.numpy as jnp
        import numpy as np
        B, S, D_IN, D_OUT = (4, 64, 512, 512)
        key = jax.random.key(seed)
        k1, k2, k3, k4, k5 = jax.random.split(key, 5)
        hidden_states = jax.random.normal(k1, (B, S, D_IN), dtype=jnp.float32)
        W = jax.random.normal(k2, (D_OUT, D_IN), dtype=jnp.float32) * 0.02
        b = jax.random.normal(k3, (D_OUT,), dtype=jnp.float32) * 0.02
        coeff = jax.random.normal(k4, (B,), dtype=jnp.float32) * 0.01
        mask = jax.random.randint(k5, (B, D_IN, D_OUT), 0, 2, dtype=jnp.int32)
        return {'hidden_states': hidden_states, 'W': W, 'b': b, 'coeff': coeff, 'mask': mask}
    _L1_cond_all = _L1_cond_setup()
    _L1_cond_in = {k: v for k, v in _L1_cond_all.items() if k in ('W', 'b')}
    del _L1_cond_all

    def _L2_cond_setup():
        import jax, jax.numpy as jnp
        import numpy as np
        RANK = 16
        ALPHA = 16.0
        SCALING = ALPHA / RANK
        N_ADAPTERS = 8
        IN_F = 512
        OUT_F = 512
        BATCH = 4
        SEQ = 256
        key = jax.random.key(seed)
        kx, ka, kb, ki = jax.random.split(key, 4)
        x = jax.random.normal(kx, (BATCH, SEQ, IN_F), dtype=jnp.float32)
        A = jax.random.normal(ka, (N_ADAPTERS, OUT_F, RANK), dtype=jnp.float32) * 0.02
        B = jax.random.normal(kb, (N_ADAPTERS, RANK, IN_F), dtype=jnp.float32) * 0.02
        adapter_ids = jax.random.randint(ki, (BATCH,), 0, N_ADAPTERS, dtype=jnp.int32)
        return {'x': x, 'A': A, 'B': B, 'adapter_ids': adapter_ids}
    _L2_cond_all = _L2_cond_setup()
    _L2_cond_in = {k: v for k, v in _L2_cond_all.items() if k in ('A', 'B')}
    del _L2_cond_all

    def _L3_cond_setup():
        import jax, jax.numpy as jnp
        import numpy as np
        B, S, D_IN, D_OUT = (4, 256, 512, 512)
        R, NUM_LABELERS = (32, 5)
        LORA_SCALING = 16 / 32
        key = jax.random.key(seed)
        k1, k2, k3, k4, k5 = jax.random.split(key, 5)
        x = jax.random.normal(k1, (B, S, D_IN), dtype=jnp.float32)
        labeler_index = jax.random.randint(k2, (B,), 0, NUM_LABELERS, dtype=jnp.int64)
        W = jax.random.normal(k3, (D_OUT, D_IN), dtype=jnp.float32) * 0.02
        lora_A = jax.random.normal(k4, (NUM_LABELERS, D_IN, R), dtype=jnp.float32) * 0.02
        lora_B_w = jax.random.normal(k5, (D_OUT, R), dtype=jnp.float32) * 0.02
        return {'x': x, 'labeler_index': labeler_index, 'W': W, 'lora_A': lora_A, 'lora_B_w': lora_B_w}
    _L3_cond_all = _L3_cond_setup()
    _L3_cond_in = {k: v for k, v in _L3_cond_all.items() if k in ('W', 'lora_A', 'lora_B_w')}
    del _L3_cond_all
    return {'x': x, 'itok_B_0_15': itok_B_0_15, 'condB_coeff': condB_coeff, 'itok_B_3_7': itok_B_3_7, 'itok_B_0_2': itok_B_0_2, 'mask_Bx4096x4096_ik1': mask_Bx4096x4096_ik1, 'L0_cond_W': _L0_cond_in['W'], 'L0_cond_lora_A': _L0_cond_in['lora_A'], 'L0_cond_lora_B': _L0_cond_in['lora_B'], 'L1_cond_W': _L1_cond_in['W'], 'L1_cond_b': _L1_cond_in['b'], 'L2_cond_A': _L2_cond_in['A'], 'L2_cond_B': _L2_cond_in['B'], 'L3_cond_W': _L3_cond_in['W'], 'L3_cond_lora_A': _L3_cond_in['lora_A'], 'L3_cond_lora_B_w': _L3_cond_in['lora_B_w']}

def reference(x, itok_B_0_15, condB_coeff, itok_B_3_7, itok_B_0_2, mask_Bx4096x4096_ik1, L0_cond_W, L0_cond_lora_A, L0_cond_lora_B, L1_cond_W, L1_cond_b, L2_cond_A, L2_cond_B, L3_cond_W, L3_cond_lora_A, L3_cond_lora_B_w):
    import jax
    import jax.numpy as jnp

    def _L0_cond_ref(x, adapter_indices, W, lora_A, lora_B):
        import jax, jax.numpy as jnp
        import numpy as np
        SCALING = 16.0 / 16
        base_out = jnp.einsum('bsi,io->bso', x, W)
        A = lora_A[adapter_indices]
        Bm = lora_B[adapter_indices]
        xr = jnp.einsum('bsi,bir->bsr', x, A)
        lora_out = jnp.einsum('bsr,bro->bso', xr, Bm)
        return base_out + lora_out * SCALING

    def _L1_cond_ref(hidden_states, W, b, coeff, mask):
        import jax, jax.numpy as jnp
        import numpy as np
        B, S, D_IN, D_OUT = (4, 64, 512, 512)
        output = jnp.einsum('bsi,oi->bso', hidden_states, W) + b
        sign = (2 * mask - 1).astype(hidden_states.dtype)
        diff = jnp.einsum('bsi,bio->bso', hidden_states, sign)
        return output + diff * coeff[:, None, None]

    def _L2_cond_ref(x, A, B, adapter_ids):
        import jax, jax.numpy as jnp
        import numpy as np
        RANK = 16
        ALPHA = 16.0
        SCALING = ALPHA / RANK
        N_ADAPTERS = 8
        IN_F = 512
        OUT_F = 512
        BATCH = 4
        SEQ = 256
        B_sel = B[adapter_ids]
        A_sel = A[adapter_ids]
        Bx = jnp.einsum('bni,bri->bnr', x, B_sel)
        out = jnp.einsum('bnr,bor->bno', Bx, A_sel)
        return out * SCALING

    def _L3_cond_ref(x, labeler_index, W, lora_A, lora_B_w):
        import jax, jax.numpy as jnp
        import numpy as np
        B, S, D_IN, D_OUT = (4, 256, 512, 512)
        R, NUM_LABELERS = (32, 5)
        LORA_SCALING = 16 / 32
        base = jnp.einsum('bsi,oi->bso', x, W)
        labelers_A = lora_A[labeler_index]
        low = jnp.einsum('bsi,bir->bsr', x, labelers_A)
        delta = jnp.einsum('bsr,or->bso', low, lora_B_w) * LORA_SCALING
        return base + delta
    x = x + _L0_cond_ref(x, itok_B_0_15, L0_cond_W, L0_cond_lora_A, L0_cond_lora_B)
    x = x + _L1_cond_ref(x, L1_cond_W, L1_cond_b, condB_coeff, mask_Bx4096x4096_ik1)
    x = x + _L2_cond_ref(x, L2_cond_A, L2_cond_B, itok_B_3_7)
    x = x + _L3_cond_ref(x, itok_B_0_2, L3_cond_W, L3_cond_lora_A, L3_cond_lora_B_w)
    return x

_drawn_inputs = setup_inputs


def setup_inputs(seed=0):
    import zlib

    import numpy as np

    out = dict(_drawn_inputs(seed))
    spreads = {}
    factors = {'L1_cond_b': 3.687, 'L3_cond_lora_A': 2.709, 'L3_cond_lora_B_w': 2.677}
    for name, (base, spread) in spreads.items():
        noise = np.random.default_rng([zlib.crc32(name.encode()), seed]).standard_normal(out[name].shape)
        drawn = base * np.exp(spread * noise) if base else spread * noise
        out[name] = jnp.asarray(drawn.astype(out[name].dtype))
    for name, factor in factors.items():
        out[name] = (out[name] * factor).astype(out[name].dtype)
    return out
```

```python
from contextlib import ExitStack

import concourse.bass as bass
from concourse import mybir

F32 = mybir.dt.float32
F32R = mybir.dt.float32r
I32 = mybir.dt.int32
ALU = mybir.AluOpType
ACT = mybir.ActivationFunctionType


def build(nc, x, idx0, coeff, idx2, idx3, mask, W0, A0, B0, W1, bias, A2, B2, W3, A3, Bw, out):
    P = 128
    NB, S, D = x.shape
    C = D // P
    PAIRS = NB // 2
    R0 = A0.shape[2]
    R2 = A2.shape[2]
    R3 = A3.shape[2]
    HALF = P // 2
    assert S == P and R0 == 16 and R2 == 16 and R3 == 32 and NB * R2 == P

    ctx = ExitStack()
    with ctx:
        def sb(name, shape, dt=F32):
            return ctx.enter_context(nc.sbuf_tensor(name, shape, dt))

        def ps(name, shape):
            return ctx.enter_context(nc.psum_tensor(name, shape, F32))

        def sem(name):
            return ctx.enter_context(nc.semaphore(name))

        def f32(ap):
            return ap.bitcast(F32)

        x_nat = sb("x_nat", [P, 2, 2, D])
        stage_a = sb("stage_a", [P, C, D])
        stage_b = sb("stage_b", [P, C, D])
        w0_hi, w0_lo = sb("w0_hi", [P, C, D], F32R), sb("w0_lo", [P, C, D], F32R)
        w1_t = sb("w1_t", [P, C, D])
        w3_hi, w3_lo = sb("w3_hi", [P, C, D], F32R), sb("w3_lo", [P, C, D], F32R)
        xt_hi, xt_lo = sb("xt_hi", [P, C, 2 * P], F32R), sb("xt_lo", [P, C, 2 * P], F32R)
        x1_hi, x1_lo = sb("x1_hi", [P, C, 2 * P], F32R), sb("x1_lo", [P, C, 2 * P], F32R)
        x2_hi, x2_lo = sb("x2_hi", [P, C, 2 * P], F32R), sb("x2_lo", [P, C, 2 * P], F32R)
        x2_nat = sb("x2_nat", [P, 2, D])
        mix = sb("mix", [P, 2, C, D])
        m_hi, m_lo = sb("m_hi", [P, 2, C, D], F32R), sb("m_lo", [P, 2, C, D], F32R)
        a0 = sb("a0", [P, C, NB, R0])
        a0_st = sb("a0_st", [P, C, NB, 2, 2, R0], F32R)
        b0 = sb("b0", [P, 2, D])
        b0_hi, b0_lo = sb("b0_hi", [P, 2, D], F32R), sb("b0_lo", [P, 2, D], F32R)
        xr = sb("xr", [P, 2 * P], F32R)
        xr_st = sb("xr_st", [P, 2 * P], F32R)
        a2_hi, a2_lo = sb("a2_hi", [P, C, P], F32R), sb("a2_lo", [P, C, P], F32R)
        d_hi, d_lo = sb("d_hi", [P, C, NB, HALF], F32R), sb("d_lo", [P, C, NB, HALF], F32R)
        uw_st = sb("uw_st", [P, 2, P], F32R)
        bw_t = sb("bw_t", [P, D])
        h_t = sb("h_t", [P, 2, P])
        same = sb("same", [P, 2, P])
        g_hl = sb("g_hl", [P, 2, D], F32R)
        up = sb("up", [P, 2, 2, D], F32R)
        ident = sb("ident", [P, P])
        bias_bc = sb("bias_bc", [P, D])
        c_bc = sb("c_bc", [P, NB])
        c_two = sb("c_two", [P, NB])
        c_neg = sb("c_neg", [P, NB])
        lo_row = sb("lo_row", [P, 1])
        idx_sb = sb("idx_sb", [1, 3, NB], I32)

        a2 = stage_a[:, 0, :].rearrange("p (k n) -> p k n", k=C)
        b2 = stage_a[:, 1, :]
        a3 = stage_a[:, 2:4, :].rearrange("p a n -> p (a n)").rearrange("p (k n) -> p k n", k=C)
        bw_rep = x2_nat[:, 0, :].rearrange("p (q n) -> p q n", q=C)

        p_tr = [ps(f"p_tr{i}", [P, D]) for i in range(2)]
        p_l0 = ps("p_l0", [P, C, 2 * P])
        p_l1 = ps("p_l1", [P, D])
        p_dn = ps("p_dn", [P, 2, 2 * P])
        p_out = [ps(f"p_out{i}", [P, D]) for i in range(2)]

        in_idx, in_small, in_bw = sem("in_idx"), sem("in_small"), sem("in_bw")
        in_x = [sem(f"in_x{i}") for i in range(2)]
        in_w0, in_w1, in_w3 = sem("in_w0"), sem("in_w1"), sem("in_w3")
        in_mask = [sem(f"in_mask{i}") for i in range(2)]
        in_a0 = sem("in_a0")
        in_b0 = [sem(f"in_b0{i}") for i in range(2)]
        in_adapt, in_up = sem("in_adapt"), sem("in_up")
        stored = [sem(f"stored{i}") for i in range(C)]
        ident_ok, const_ok, zero_ok, fill_ok = sem("ident_ok"), sem("const_ok"), sem("zero_ok"), sem("fill_ok")
        w0_diag, w1_diag, w3_diag = sem("w0_diag"), sem("w1_diag"), sem("w3_diag")
        w0h_ok, w0l_ok, w3h_ok, w3l_ok = sem("w0h_ok"), sem("w0l_ok"), sem("w3h_ok"), sem("w3l_ok")
        tr_full, tr_act, tr_dve = sem("tr_full"), sem("tr_act"), sem("tr_dve")
        a0h_ok, a0l_ok = sem("a0h_ok"), sem("a0l_ok")
        b0h_ok, b0l_ok = sem("b0h_ok"), sem("b0l_ok")
        dn0_full, xr_ok, xrst_ok = sem("dn0_full"), sem("xr_ok"), sem("xrst_ok")
        l0_full, x1h_ok, x1l_ok = sem("l0_full"), sem("x1h_ok"), sem("x1l_ok")
        sign_ok, mix_ok, mh_ok, ml_ok = sem("sign_ok"), sem("mix_ok"), sem("mh_ok"), sem("ml_ok")
        l1_full, x2_ok = sem("l1_full"), sem("x2_ok")
        dn2_full, uwh_ok, uwl_ok = sem("dn2_full"), sem("uwh_ok"), sem("uwl_ok")
        out_full, out_ok = sem("out_full"), sem("out_ok")
        adapt_h, adapt_l = sem("adapt_h"), sem("adapt_l")
        ht_full, ht_ok, g_full, gh_ok, gl_ok = (sem(n) for n in ("ht_full", "ht_ok", "g_full", "gh_ok", "gl_ok"))
        upc_h, upc_l = sem("upc_h"), sem("upc_l")

        USES = [("x", 0), ("x", 1), ("bw", 0)] + [("w1", c) for c in range(C)] + [("x", 2), ("x", 3)]
        for p in range(PAIRS):
            if p == 0:
                USES += [("w3", c) for c in range(C)]
            USES += [("x2", 2 * p), ("x2", 2 * p + 1)]
            if p + 2 < PAIRS:
                USES += [("x", 2 * p + 4), ("x", 2 * p + 5)]
            if p == 0:
                USES += [("b2", 0)]
        BOTH = ("x", "x2", "b2")

        def use(kind, i):
            return USES.index((kind, i))

        def dve_reads(n):
            return sum(k in BOTH for k, _ in USES[:n + 1])

        block = ctx.enter_context(nc.Block())

        @block.sync
        def _(sp):
            for i, t in enumerate((idx0, idx2, idx3)):
                sp.dma_start(idx_sb[0:1, i, :], t.rearrange("(a n) -> a n", a=1)).then_inc(in_idx, 16)

            def load_x(p):
                if p >= 2:
                    sp.wait_ge(tr_full, use("x", 2 * (p - 2) + 1) + 1)
                sp.dma_start(x_nat[:, p % 2], x[2 * p:2 * p + 2].rearrange("b t d -> t b d")).then_inc(in_x[p % 2], 16)

            def load_mask(b):
                if b >= 2:
                    sp.wait_ge(ml_ok, b - 1)
                sp.dma_start(mix[:, b % 2].bitcast(I32), mask[b].rearrange("(c p) o -> p c o", p=P)).then_inc(in_mask[b % 2], 16)

            load_x(0)
            sp.dma_start(stage_a[:], W0.rearrange("(c p) o -> p c o", p=P)).then_inc(in_w0, 16)
            sp.dma_start(stage_b[:], W1.rearrange("(q p) i -> p q i", p=P)).then_inc(in_w1, 16)
            load_mask(0)
            load_x(1)
            load_mask(1)
            sp.wait_ge(w0l_ok, 2)
            sp.dma_start(stage_a[:], W3.rearrange("(q p) i -> p q i", p=P)).then_inc(in_w3, 16)
            load_mask(2)
            load_mask(3)
            for p in range(PAIRS):
                if p + 2 < PAIRS:
                    load_x(p + 2)
                    load_mask(2 * p + 4)
                    load_mask(2 * p + 5)
                sp.wait_ge(gl_ok, 1)
                sp.wait_ge(fill_ok, 1)
                if p >= 1:
                    sp.wait_ge(out_full, 2 * p)
                for s in range(2):
                    b = 2 * p + s
                    for h in range(2):
                        sp.dma_start(f32(up[h * HALF:h * HALF + R2, s]),
                                     f32(g_hl[b * R2:(b + 1) * R2, :, :])).then_inc(in_up, 16)
                if p >= 1:
                    for b in (2 * p - 2, 2 * p - 1):
                        sp.wait_ge(out_ok, b + 1)
                        sp.dma_start(out[b], stage_b[:, b % C]).then_inc(stored[b % C], 16)
            for b in (NB - 2, NB - 1):
                sp.wait_ge(out_ok, b + 1)
                sp.dma_start(out[b], stage_b[:, b % C]).then_inc(stored[b % C], 16)
            for i in range(C):
                sp.wait_ge(stored[i], 16 * (NB // C))

        @block.gpsimd
        def _(pool):
            pool.memset(ident[:], 0.0).then_inc(zero_ok, 1)
            pool.wait_ge(zero_ok, 1)
            pool.affine_select(out=ident[:], in_=ident[:], compare_op=ALU.not_equal, fill=1.0, base=0,
                               pattern=[[-1, P]], channel_multiplier=1).then_inc(ident_ok, 1)
            pool.memset(f32(xr_st[:]), 0.0).then_inc(const_ok, 1)
            pool.memset(lo_row[:], 0.0).then_inc(const_ok, 1)
            pool.wait_ge(const_ok, 2)
            for s in range(2):
                pool.memset(lo_row[s * HALF + 32:s * HALF + 64], -1.0).then_inc(const_ok, 1)

            pool.wait_ge(in_idx, 48)

            def load_index(t, last):
                return [pool.value_load(idx_sb[0:1, t, b:b + 1], min_val=0, max_val=last) for b in range(NB)]

            i0 = load_index(0, A0.shape[0] - 1)
            for b in range(NB):
                pool.dma_start(a0[:, :, b, :], A0[bass.ds(i0[b], 1)].rearrange("a (c p) r -> p (a c) r", p=P)).then_inc(in_a0, 16)

            def load_b0(p):
                if p >= 2:
                    pool.wait_ge(b0l_ok, p - 1)
                for s in range(2):
                    src = B0[bass.ds(i0[2 * p + s], 1)].rearrange("a r o -> (a r) o")
                    for k in range(4):
                        at = s * HALF + k * R0
                        pool.dma_start(b0[at:at + R0, p % 2], src).then_inc(in_b0[p % 2], 16)

            load_b0(0)
            load_b0(1)
            pool.wait_ge(in_small, 32)
            pool.wait_ge(const_ok, 4)
            pool.tensor_scalar(c_two[:], c_bc[:], 2.0, None, ALU.mult).then_inc(const_ok, 1)
            pool.tensor_scalar(c_neg[:], c_bc[:], -1.0, None, ALU.mult).then_inc(const_ok, 1)

            def add_identity(t, c, done):
                at = t[:, c, c * P:(c + 1) * P]
                pool.tensor_tensor(at, at, ident[:], ALU.add).then_inc(done, 1)

            pool.wait_ge(ident_ok, 1)
            pool.wait_ge(in_w0, 16)
            for c in range(C):
                add_identity(stage_a, c, w0_diag)
            for c in range(C):
                pool.wait_ge(tr_act, use("w1", c) + 1)
                add_identity(w1_t, c, w1_diag)

            pool.memset(same[:], 1.0).then_inc(zero_ok, 1)
            pool.memset(f32(d_hi[:]), 0.0).then_inc(zero_ok, 1)
            pool.memset(f32(d_lo[:]), 0.0).then_inc(zero_ok, 1)
            pool.memset(f32(up[:]), 0.0).then_inc(zero_ok, 1)
            pool.wait_ge(zero_ok, 5)
            for step, side in enumerate((1, -1)):
                for g in range(2):
                    pool.affine_select(out=same[:, g, :].rearrange("p (b r) -> p b r", r=R2),
                                       in_=same[:, g, :].rearrange("p (b r) -> p b r", r=R2),
                                       compare_op=ALU.is_ge, fill=0.0,
                                       base=side * 4 * g * R3 + (R3 - 1 if side < 0 else 0),
                                       pattern=[[-side * R3, NB], [0, R2]],
                                       channel_multiplier=side).then_inc(fill_ok, 1)
                if step == 0:
                    pool.wait_ge(fill_ok, 2)
            for c in range(C):
                pool.wait_ge(tr_act, use("w3", c) + 1)
                add_identity(stage_b, c, w3_diag)
            pool.wait_ge(tr_full, use("w3", C - 1) + 1)
            i2 = load_index(1, A2.shape[0] - 1)
            i3 = load_index(2, A3.shape[0] - 1)
            for b in range(NB):
                pool.dma_start(b2[b * R2:(b + 1) * R2, :], B2[bass.ds(i2[b], 1)].rearrange("a r i -> (a r) i")).then_inc(in_adapt, 16)
                pool.dma_start(a2[:, :, b * R2:(b + 1) * R2], A2[bass.ds(i2[b], 1)].rearrange("a (k p) r -> p (a k) r", p=P)).then_inc(in_adapt, 16)
                pool.dma_start(a3[:, :, b * R3:(b + 1) * R3], A3[bass.ds(i3[b], 1)].rearrange("a (k p) r -> p (a k) r", p=P)).then_inc(in_adapt, 16)
            for p in range(2, PAIRS):
                load_b0(p)

        @block.scalar
        def _(act):
            act.dma_start(c_bc[:], coeff.rearrange("(a n) -> a n", a=1).to_broadcast([P, NB])).then_inc(in_small, 16)
            act.dma_start(bias_bc[:], bias.rearrange("(a n) -> a n", a=1).to_broadcast([P, D])).then_inc(in_small, 16)
            for k in range(4):
                act.dma_start(bw_rep[:, :, k * R3:(k + 1) * R3], Bw.rearrange("(q p) r -> p q r", p=P)).then_inc(in_bw, 16)

            def cp(o, i, **kw):
                return nc.scalar.activation(o, i, ACT.Copy, **kw)

            def transposed_hi(kind, b, dst):
                n = use(kind, b)
                act.wait_ge(tr_full, n + 1)
                s = b % 2
                cp(dst[:, :, s * P:(s + 1) * P], p_tr[n % 2][:].rearrange("p (c t) -> p c t", c=C)).then_inc(tr_act, 1)

            def x1_high(p, h):
                act.wait_ge(l0_full, 2 * p + h + 1)
                cp(x1_hi[:, 2 * h:2 * h + 2, :], p_l0[:, 2 * h:2 * h + 2, :]).then_inc(x1h_ok, 1)

            def b0_high(p):
                act.wait_ge(in_b0[p % 2], 128 * (p // 2 + 1))
                if p >= 2:
                    act.wait_ge(l0_full, 2 * (p - 1))
                cp(b0_hi[:, p % 2], b0[:, p % 2]).then_inc(b0h_ok, 1)

            def xr_high(p):
                act.wait_ge(dn0_full, p + 1)
                if p >= 1:
                    act.wait_ge(xrst_ok, 2 * p)
                cp(xr[:], p_dn[:, 0]).then_inc(xr_ok, 1)

            def sign_times_c(b):
                act.wait_ge(in_mask[b % 2], 16 * (b // 2 + 1))
                nc.scalar.activation(mix[:, b % 2], mix[:, b % 2].bitcast(I32), ACT.Identity,
                                     scale=c_two[:, b:b + 1], bias=c_neg[:, b:b + 1]).then_inc(sign_ok, 1)

            def m_high(b):
                act.wait_ge(mix_ok, b + 1)
                if b >= 2:
                    act.wait_ge(l1_full, b - 1)
                cp(m_hi[:, b % 2], mix[:, b % 2]).then_inc(mh_ok, 1)

            def uw_high(b):
                s = b % 2
                act.wait_ge(dn2_full, b // 2 + 1)
                rows = slice(s * HALF, (s + 1) * HALF)
                cp(uw_st[rows, s, :], p_dn[rows, 1, s * P:(s + 1) * P]).then_inc(uwh_ok, 1)

            def out_copy(b):
                act.wait_ge(out_full, b + 1)
                if b == 0:
                    act.wait_ge(w3l_ok, 1)
                if b >= C:
                    act.wait_ge(stored[b % C], 16 * (b // C))
                cp(stage_b[:, b % C], p_out[b % 2][:]).then_inc(out_ok, 1)

            transposed_hi("x", 0, xt_hi)
            transposed_hi("x", 1, xt_hi)
            act.wait_ge(tr_full, use("bw", 0) + 1)
            cp(bw_t[:], p_tr[use("bw", 0) % 2][:], scale=0.5).then_inc(tr_act, 1)
            act.wait_ge(in_a0, 16 * NB)
            for rep in range(2):
                cp(a0_st[:, :, :, rep, 0, :].rearrange("p c b r -> p (c b) r"),
                   a0[:].rearrange("p c b r -> p (c b) r")).then_inc(a0h_ok, 1)
            for h in range(2):
                act.wait_ge(w0_diag, 2 * h + 2)
                cp(w0_hi[:, 2 * h:2 * h + 2], stage_a[:, 2 * h:2 * h + 2]).then_inc(w0h_ok, 1)
            xr_high(0)
            b0_high(0)
            for c in range(C):
                n = use("w1", c)
                act.wait_ge(tr_full, n + 1)
                cp(w1_t[:, c], p_tr[n % 2][:]).then_inc(tr_act, 1)
            act.wait_ge(const_ok, 6)
            sign_times_c(0)
            x1_high(0, 0)
            m_high(0)
            x1_high(0, 1)
            transposed_hi("x", 2, xt_hi)
            transposed_hi("x", 3, xt_hi)
            sign_times_c(1)
            m_high(1)
            b0_high(1)
            sign_times_c(2)
            sign_times_c(3)
            for p in range(PAIRS):
                last = p == PAIRS - 1
                if not last:
                    m_high(2 * p + 2)
                if p >= 1:
                    uw_high(2 * p - 2)
                    uw_high(2 * p - 1)
                if p == 0:
                    for c in range(C):
                        n = use("w3", c)
                        act.wait_ge(tr_full, n + 1)
                        cp(stage_b[:, c], p_tr[n % 2][:]).then_inc(tr_act, 1)
                if not last:
                    xr_high(p + 1)
                    m_high(2 * p + 3)
                    if p + 2 < PAIRS:
                        b0_high(p + 2)
                    x1_high(p + 1, 0)
                    x1_high(p + 1, 1)
                if p == 0:
                    act.wait_ge(w3_diag, C)
                    cp(w3_hi[:], stage_b[:]).then_inc(w3h_ok, 1)
                if p >= 1:
                    out_copy(2 * p - 2)
                if p + 2 < PAIRS:
                    sign_times_c(2 * p + 4)
                if p >= 1:
                    out_copy(2 * p - 1)
                if p + 2 < PAIRS:
                    sign_times_c(2 * p + 5)
                transposed_hi("x2", 2 * p, x2_hi)
                transposed_hi("x2", 2 * p + 1, x2_hi)
                if p + 2 < PAIRS:
                    transposed_hi("x", 2 * p + 4, xt_hi)
                    transposed_hi("x", 2 * p + 5, xt_hi)
                if p == 0:
                    act.wait_ge(in_adapt, 16 * 3 * NB)
                    act.wait_ge(zero_ok, 5)
                    cp(a2_hi[:], a2).then_inc(adapt_h, 1)
                    cp(d_hi[:, :, :, 32:64].rearrange("p c b r -> p (c b) r"),
                       a3.rearrange("p c (b r) -> p (c b) r", r=R3)).then_inc(adapt_h, 1)
                    for h in range(2):
                        rows = slice(h * HALF + 32, h * HALF + 64)
                        for s in range(2):
                            cp(up[rows, s, 0], bw_t[rows, :]).then_inc(upc_h, 1)
                    n = use("b2", 0)
                    act.wait_ge(tr_full, n + 1)
                    cp(d_hi[:, :, :, 0:R2].rearrange("p c b r -> p (c b) r"),
                       p_tr[n % 2][:].rearrange("p (c b r) -> p (c b) r", c=C, r=R2)).then_inc(tr_act, 1)
                    act.wait_ge(g_full, 1)
                    cp(g_hl[:, 0], p_out[0][:]).then_inc(gh_ok, 1)
            uw_high(NB - 2)
            uw_high(NB - 1)
            out_copy(NB - 2)
            out_copy(NB - 1)

        @block.vector
        def _(dve):
            def lo(o, full, hi):
                return nc.vector.tensor_tensor(o, full, f32(hi), ALU.subtract)

            def transposed_lo(kind, b, hi, dst):
                n = use(kind, b)
                dve.wait_ge(tr_act, n + 1)
                cols = slice((b % 2) * P, (b % 2 + 1) * P)
                lo(dst[:, :, cols], p_tr[n % 2][:].rearrange("p (c t) -> p c t", c=C), hi[:, :, cols]).then_inc(tr_dve, 1)

            def x1_low(p, h):
                dve.wait_ge(x1h_ok, 2 * p + h + 1)
                at = slice(2 * h, 2 * h + 2)
                lo(x1_lo[:, at], p_l0[:, at], x1_hi[:, at]).then_inc(x1l_ok, 1)

            def b0_low(p):
                dve.wait_ge(b0h_ok, p + 1)
                lo(b0_lo[:, p % 2], b0[:, p % 2], b0_hi[:, p % 2]).then_inc(b0l_ok, 1)

            def xr_stack(p):
                dve.wait_ge(xr_ok, p + 1)
                for s in range(2):
                    rows, cols = slice(s * HALF, (s + 1) * HALF), slice(s * P, (s + 1) * P)
                    nc.vector.scalar_tensor_tensor(xr_st[rows, cols], f32(xr[rows, cols]), lo_row[rows, 0:1],
                                                   p_dn[rows, 0, cols], ALU.mult, ALU.add).then_inc(xrst_ok, 1)

            def mix_weights(b):
                dve.wait_ge(sign_ok, b + 1)
                nc.vector.tensor_tensor(mix[:, b % 2], mix[:, b % 2], w1_t[:], ALU.add).then_inc(mix_ok, 1)

            def m_low(b):
                dve.wait_ge(mh_ok, b + 1)
                lo(m_lo[:, b % 2], mix[:, b % 2], m_hi[:, b % 2]).then_inc(ml_ok, 1)

            def x2_bias(b):
                dve.wait_ge(l1_full, b + 1)
                nc.vector.tensor_tensor(x2_nat[:, b % 2], p_l1[:], bias_bc[:], ALU.add).then_inc(x2_ok, 1)

            def uw_low(b):
                s = b % 2
                dve.wait_ge(uwh_ok, b + 1)
                rows, other = slice(s * HALF, (s + 1) * HALF), slice((1 - s) * HALF, (2 - s) * HALF)
                lo(uw_st[other, s, :], p_dn[rows, 1, s * P:(s + 1) * P], uw_st[rows, s, :]).then_inc(uwl_ok, 1)

            transposed_lo("x", 0, xt_hi, xt_lo)
            transposed_lo("x", 1, xt_hi, xt_lo)
            for rep in range(2):
                dve.wait_ge(a0h_ok, rep + 1)
                lo(a0_st[:, :, :, rep, 1, :].rearrange("p c b r -> p (c b) r"),
                   a0[:].rearrange("p c b r -> p (c b) r"),
                   a0_st[:, :, :, rep, 0, :].rearrange("p c b r -> p (c b) r")).then_inc(a0l_ok, 1)
            for h in range(2):
                dve.wait_ge(w0h_ok, h + 1)
                at = slice(2 * h, 2 * h + 2)
                lo(w0_lo[:, at], stage_a[:, at], w0_hi[:, at]).then_inc(w0l_ok, 1)
            dve.wait_ge(const_ok, 4)
            xr_stack(0)
            b0_low(0)
            dve.wait_ge(w1_diag, C)
            mix_weights(0)
            x1_low(0, 0)
            m_low(0)
            x1_low(0, 1)
            transposed_lo("x", 2, xt_hi, xt_lo)
            transposed_lo("x", 3, xt_hi, xt_lo)
            mix_weights(1)
            m_low(1)
            b0_low(1)
            mix_weights(2)
            mix_weights(3)
            dve.wait_ge(in_small, 32)
            for p in range(PAIRS):
                last = p == PAIRS - 1
                x2_bias(2 * p)
                if not last:
                    m_low(2 * p + 2)
                if p >= 1:
                    uw_low(2 * p - 2)
                    uw_low(2 * p - 1)
                x2_bias(2 * p + 1)
                if not last:
                    xr_stack(p + 1)
                    m_low(2 * p + 3)
                    if p + 2 < PAIRS:
                        b0_low(p + 2)
                    x1_low(p + 1, 0)
                    x1_low(p + 1, 1)
                if p == 0:
                    dve.wait_ge(w3h_ok, 1)
                    lo(w3_lo[:], stage_b[:], w3_hi[:]).then_inc(w3l_ok, 1)
                if p + 2 < PAIRS:
                    mix_weights(2 * p + 4)
                    mix_weights(2 * p + 5)
                transposed_lo("x2", 2 * p, x2_hi, x2_lo)
                transposed_lo("x2", 2 * p + 1, x2_hi, x2_lo)
                if p + 2 < PAIRS:
                    transposed_lo("x", 2 * p + 4, xt_hi, xt_lo)
                    transposed_lo("x", 2 * p + 5, xt_hi, xt_lo)
                if p == 0:
                    dve.wait_ge(adapt_h, 1)
                    lo(a2_lo[:], a2, a2_hi[:]).then_inc(adapt_l, 1)
                    dve.wait_ge(adapt_h, 2)
                    lo(d_lo[:, :, :, 32:64].rearrange("p c b r -> p (c b) r"),
                       a3.rearrange("p c (b r) -> p (c b) r", r=R3),
                       d_hi[:, :, :, 32:64].rearrange("p c b r -> p (c b) r")).then_inc(adapt_l, 1)
                    for h in range(2):
                        rows = slice(h * HALF + 32, h * HALF + 64)
                        for s in range(2):
                            dve.wait_ge(upc_h, 2 * h + s + 1)
                            lo(up[rows, s, 1], bw_t[rows, :], up[rows, s, 0]).then_inc(upc_l, 1)
                    n = use("b2", 0)
                    dve.wait_ge(tr_act, n + 1)
                    lo(d_lo[:, :, :, 0:R2].rearrange("p c b r -> p (c b) r"),
                       p_tr[n % 2][:].rearrange("p (c b r) -> p (c b) r", c=C, r=R2),
                       d_hi[:, :, :, 0:R2].rearrange("p c b r -> p (c b) r")).then_inc(tr_dve, 1)
                    dve.wait_ge(ht_full, 1)
                    dve.wait_ge(fill_ok, 4)
                    nc.vector.tensor_tensor(h_t[:].rearrange("p g n -> p (g n)"), p_out[1][:, 0:2 * P],
                                            same[:].rearrange("p g n -> p (g n)"), ALU.mult).then_inc(ht_ok, 1)
                    dve.wait_ge(gh_ok, 1)
                    lo(g_hl[:, 1], p_out[0][:], g_hl[:, 0]).then_inc(gl_ok, 1)
            uw_low(NB - 2)
            uw_low(NB - 1)

        @block.tensor
        def _(pe):
            mm = nc.tensor.matmul

            def bank_free(n):
                if n >= 2:
                    pe.wait_ge(tr_act, n - 1)
                    if dve_reads(n - 2):
                        pe.wait_ge(tr_dve, dve_reads(n - 2))

            def transpose4(kind, i, blocks):
                n = use(kind, i)
                bank_free(n)
                for c in range(C):
                    t = nc.tensor.transpose(p_tr[n % 2][:, c * P:(c + 1) * P], blocks(c), ident[:])
                t.then_inc(tr_full, 1)

            def transpose_x(b):
                pe.wait_ge(in_x[b // 2 % 2], 16 * (b // 4 + 1))
                transpose4("x", b, lambda c: x_nat[:, b // 2 % 2, b % 2, c * P:(c + 1) * P])

            def transpose_x2(b):
                pe.wait_ge(x2_ok, b + 1)
                transpose4("x2", b, lambda c: x2_nat[:, b % 2, c * P:(c + 1) * P])

            def down0(p):
                pe.wait_ge(tr_act, use("x", 2 * p + 1) + 1)
                pe.wait_ge(tr_dve, dve_reads(use("x", 2 * p + 1)))
                if p == 0:
                    pe.wait_ge(a0l_ok, 2)
                else:
                    pe.wait_ge(xrst_ok, 2 * p)
                if p >= 2:
                    pe.wait_ge(uwl_ok, 2 * (p - 1))
                for c in range(C):
                    w = a0_st[:, c, 2 * p:2 * p + 2].rearrange("p b e h r -> p (b e h r)")
                    mm(p_dn[:, 0], w, xt_hi[:, c], start=(c == 0), stop=False)
                    t = mm(p_dn[:, 0], w, xt_lo[:, c], start=False, stop=(c == C - 1))
                t.then_inc(dn0_full, 1)

            def layer0(p):
                if p == 0:
                    pe.wait_ge(w0l_ok, 2)
                else:
                    pe.wait_ge(x1l_ok, 2 * p)
                for q in range(C):
                    o = slice(q * P, (q + 1) * P)
                    for c in range(C):
                        mm(p_l0[:, q], w0_hi[:, c, o], xt_hi[:, c], start=(c == 0), stop=False)
                        mm(p_l0[:, q], w0_hi[:, c, o], xt_lo[:, c], start=False, stop=False)
                        mm(p_l0[:, q], w0_lo[:, c, o], xt_hi[:, c], start=False, stop=False)
                    if q == 0:
                        pe.wait_ge(xrst_ok, 2 * p + 2)
                        pe.wait_ge(b0l_ok, p + 1)
                    mm(p_l0[:, q], b0_hi[:, p % 2, o], xr_st[:], start=False, stop=False)
                    t = mm(p_l0[:, q], b0_lo[:, p % 2, o], xr_st[:], start=False, stop=True)
                    if q % 2:
                        t.then_inc(l0_full, 1)

            def layer1(b):
                pe.wait_ge(x1l_ok, 2 * (b // 2) + 2)
                pe.wait_ge(ml_ok, b + 1)
                if b >= 1:
                    pe.wait_ge(x2_ok, b)
                tok = slice((b % 2) * P, (b % 2 + 1) * P)
                for c in range(C):
                    mm(p_l1[:], x1_hi[:, c, tok], m_hi[:, b % 2, c], start=(c == 0), stop=False)
                    mm(p_l1[:], x1_hi[:, c, tok], m_lo[:, b % 2, c], start=False, stop=False)
                    t = mm(p_l1[:], x1_lo[:, c, tok], m_hi[:, b % 2, c], start=False, stop=(c == C - 1))
                t.then_inc(l1_full, 1)

            def down2(p):
                pe.wait_ge(tr_act, use("x2", 2 * p + 1) + 1)
                pe.wait_ge(tr_dve, dve_reads(use("x2", 2 * p + 1)))
                if p == 0:
                    pe.wait_ge(tr_dve, dve_reads(use("b2", 0)))
                    pe.wait_ge(adapt_l, 2)
                else:
                    pe.wait_ge(uwl_ok, 2 * p)
                pe.wait_ge(xrst_ok, 2 * min(p + 2, PAIRS))
                for c in range(C):
                    wh = d_hi[:, c, 2 * p:2 * p + 2].rearrange("p b r -> p (b r)")
                    wl = d_lo[:, c, 2 * p:2 * p + 2].rearrange("p b r -> p (b r)")
                    mm(p_dn[:, 1], wh, x2_hi[:, c], start=(c == 0), stop=False)
                    mm(p_dn[:, 1], wh, x2_lo[:, c], start=False, stop=False)
                    t = mm(p_dn[:, 1], wl, x2_hi[:, c], start=False, stop=(c == C - 1))
                t.then_inc(dn2_full, 1)

            def layer23(b):
                s = b % 2
                tok = slice(s * P, (s + 1) * P)
                po = p_out[b % 2]
                if b == 0:
                    pe.wait_ge(w3l_ok, 1)
                    pe.wait_ge(gl_ok, 1)
                if b >= 2:
                    pe.wait_ge(out_ok, b - 1)
                for c in range(C):
                    mm(po[:], x2_hi[:, c, tok], w3_hi[:, c], start=(c == 0), stop=False)
                    mm(po[:], x2_hi[:, c, tok], w3_lo[:, c], start=False, stop=False)
                    mm(po[:], x2_lo[:, c, tok], w3_hi[:, c], start=False, stop=False)
                pe.wait_ge(uwl_ok, b + 1)
                pe.wait_ge(in_up, 64 * (b // 2 + 1))
                if b == 0:
                    pe.wait_ge(upc_l, 4)
                mm(po[:], uw_st[:, s], up[:, s, 0], start=False, stop=False)
                mm(po[:], uw_st[:, s], up[:, s, 1], start=False, stop=True).then_inc(out_full, 1)

            def adapters():
                pe.wait_ge(in_adapt, 16 * 3 * NB)
                transpose4("b2", 0, lambda c: b2[:, c * P:(c + 1) * P])
                for g in range(2):
                    for k in range(C):
                        t = mm(p_out[1][:, g * P:(g + 1) * P], a3[:, k, g * P:(g + 1) * P], a2[:, k, :],
                               start=(k == 0), stop=(k == C - 1))
                t.then_inc(ht_full, 1)
                pe.wait_ge(adapt_l, 1)
                pe.wait_ge(w3l_ok, 1)
                for k in range(C):
                    mm(p_out[0][:], a2_hi[:, k], w3_hi[:, k], start=(k == 0), stop=False)
                    mm(p_out[0][:], a2_hi[:, k], w3_lo[:, k], start=False, stop=False)
                    mm(p_out[0][:], a2_lo[:, k], w3_hi[:, k], start=False, stop=False)
                pe.wait_ge(ht_ok, 1)
                for g in range(2):
                    t = mm(p_out[0][:], h_t[:, g], bw_t[:], start=False, stop=(g == 1))
                t.then_inc(g_full, 1)

            pe.wait_ge(ident_ok, 1)
            transpose_x(0)
            transpose_x(1)
            pe.wait_ge(in_bw, 64)
            transpose4("bw", 0, lambda c: bw_rep[:, c, :])
            down0(0)
            pe.wait_ge(in_w1, 16)
            for i in range(C):
                transpose4("w1", i, lambda q: stage_b[:, q, i * P:(i + 1) * P])
            layer0(0)
            transpose_x(2)
            transpose_x(3)
            for p in range(PAIRS):
                layer1(2 * p)
                if p >= 1:
                    down2(p - 1)
                layer1(2 * p + 1)
                if p == 0:
                    pe.wait_ge(in_w3, 16)
                    for i in range(C):
                        transpose4("w3", i, lambda q: stage_a[:, q, i * P:(i + 1) * P])
                if p + 1 < PAIRS:
                    down0(p + 1)
                    layer0(p + 1)
                if p >= 1:
                    layer23(2 * p - 2)
                    layer23(2 * p - 1)
                transpose_x2(2 * p)
                transpose_x2(2 * p + 1)
                if p + 2 < PAIRS:
                    transpose_x(2 * p + 4)
                    transpose_x(2 * p + 5)
                if p == 0:
                    adapters()
            down2(PAIRS - 1)
            layer23(NB - 2)
            layer23(NB - 1)


_INS = ["x", "itok_B_0_15", "condB_coeff", "itok_B_3_7", "itok_B_0_2", "mask_Bx4096x4096_ik1",
        "L0_cond_W", "L0_cond_lora_A", "L0_cond_lora_B", "L1_cond_W", "L1_cond_b",
        "L2_cond_A", "L2_cond_B", "L3_cond_W", "L3_cond_lora_A", "L3_cond_lora_B_w"]


def kernel(**inputs):
    import numpy as _np
    import concourse.bacc as _bacc
    from concourse import mybir as _mybir
    from concourse.bass_utils import run_bass_kernel_spmd as _run

    nc = _bacc.Bacc("TRN2", target_bir_lowering=False, num_devices=1)
    arrays, args = {}, []
    for name in _INS:
        a = _np.ascontiguousarray(inputs[name])
        arrays[f"in_{name}_dram"] = a
        args.append(nc.dram_tensor(f"in_{name}_dram", a.shape, _mybir.dt.from_np(a.dtype), kind="ExternalInput").ap())
    shape = inputs["x"].shape
    args.append(nc.dram_tensor("out_0_dram", shape, _mybir.dt.float32, kind="ExternalOutput").ap())
    build(nc, *args)
    r = _run(nc, [arrays], core_ids=[0])
    return r.results[0]["out_0_dram"]
```

```python
from contextlib import ExitStack

import concourse.bass as bass
from concourse import mybir

F32 = mybir.dt.float32
F32R = mybir.dt.float32r
I32 = mybir.dt.int32
ALU = mybir.AluOpType
ACT = mybir.ActivationFunctionType


def build(nc, x, idx0, coeff, idx2, idx3, mask, W0, A0, B0, W1, bias, A2, B2, W3, A3, Bw, out):
    P = 128
    NB, S, D = x.shape
    C = D // P
    PAIRS = NB // 2
    R0 = A0.shape[2]
    R2 = A2.shape[2]
    R3 = A3.shape[2]
    HALF = P // 2
    assert S == P and R0 == 16 and R2 == 16 and R3 == 32 and NB * R2 == P

    ctx = ExitStack()
    with ctx:
        def sb(name, shape, dt=F32):
            return ctx.enter_context(nc.sbuf_tensor(name, shape, dt))

        def ps(name, shape):
            return ctx.enter_context(nc.psum_tensor(name, shape, F32))

        def sem(name):
            return ctx.enter_context(nc.semaphore(name))

        def f32(ap):
            return ap.bitcast(F32)

        x_nat = sb("x_nat", [P, 2, 2, D])
        stage_a = sb("stage_a", [P, C, D])
        stage_b = sb("stage_b", [P, C, D])
        w0_hi, w0_lo = sb("w0_hi", [P, C, D], F32R), sb("w0_lo", [P, C, D], F32R)
        w1_t = sb("w1_t", [P, C, D])
        w3_hi, w3_lo = sb("w3_hi", [P, C, D], F32R), sb("w3_lo", [P, C, D], F32R)
        xt_hi, xt_lo = sb("xt_hi", [P, C, 2 * P], F32R), sb("xt_lo", [P, C, 2 * P], F32R)
        x1_hi, x1_lo = sb("x1_hi", [P, C, 2 * P], F32R), sb("x1_lo", [P, C, 2 * P], F32R)
        x2_hi, x2_lo = sb("x2_hi", [P, C, 2 * P], F32R), sb("x2_lo", [P, C, 2 * P], F32R)
        x2_nat = sb("x2_nat", [P, 2, D])
        mix = sb("mix", [P, 2, C, D])
        m_hi, m_lo = sb("m_hi", [P, 2, C, D], F32R), sb("m_lo", [P, 2, C, D], F32R)
        a0 = sb("a0", [P, C, NB, R0])
        b2 = sb("b2", [P, D])
        a3 = sb("a3", [P, C, NB * R3])
        a0_st = sb("a0_st", [P, C, NB, 2, 2, R0], F32R)
        b0 = sb("b0", [P, D])
        b0_hi, b0_lo = sb("b0_hi", [P, 2, D], F32R), sb("b0_lo", [P, 2, D], F32R)
        xr = sb("xr", [P, 2 * P], F32R)
        xr_st = sb("xr_st", [P, 2 * P], F32R)
        a2_hi, a2_lo = sb("a2_hi", [P, C, P], F32R), sb("a2_lo", [P, C, P], F32R)
        d_hi, d_lo = sb("d_hi", [P, C, NB, HALF], F32R), sb("d_lo", [P, C, NB, HALF], F32R)
        uw_st = sb("uw_st", [P, 2, P], F32R)
        bw_t = sb("bw_t", [P, D])
        h_t = sb("h_t", [P, 2, P])
        same = sb("same", [P, 2, P])
        g_hl = sb("g_hl", [P, 2, D], F32R)
        up = sb("up", [P, 2, 2, D], F32R)
        ident = sb("ident", [P, P])
        bias_bc = sb("bias_bc", [P, D])
        c_bc = sb("c_bc", [P, NB])
        c_two = sb("c_two", [P, NB])
        c_neg = sb("c_neg", [P, NB])
        lo_row = sb("lo_row", [P, 1])
        idx_sb = sb("idx_sb", [1, 3, NB], I32)

        a2 = a0[:].rearrange("p c b r -> p c (b r)")
        bw_nat = x2_nat[:, 1, 0:C * R3].rearrange("p (q r) -> p q r", q=C)
        bw_rep = x2_nat[:, 0, :].rearrange("p (q n) -> p q n", q=C)

        p_tr = [ps(f"p_tr{i}", [P, D]) for i in range(2)]
        p_l0 = ps("p_l0", [P, C, 2 * P])
        p_l1 = ps("p_l1", [P, D])
        p_dn = ps("p_dn", [P, 2, 2 * P])
        p_out = [ps(f"p_out{i}", [P, D]) for i in range(2)]

        in_idx0, in_idx, bw_ok = sem("in_idx0"), sem("in_idx"), sem("bw_ok")
        in_small, in_bw = sem("in_small"), sem("in_bw")
        in_x = [sem(f"in_x{i}") for i in range(2)]
        in_w0 = [sem(f"in_w0{c}") for c in range(C)]
        in_w1, in_w3 = sem("in_w1"), sem("in_w3")
        in_mask = [sem(f"in_mask{i}") for i in range(2)]
        in_a0 = sem("in_a0")
        in_b0 = sem("in_b0")
        in_a2, in_b2, in_a3, in_up = sem("in_a2"), sem("in_b2"), sem("in_a3"), sem("in_up")
        stored = [sem(f"stored{i}") for i in range(C)]
        stored_last = sem("stored_last")
        ident_ok, const_ok, zero_ok, fill_ok = sem("ident_ok"), sem("const_ok"), sem("zero_ok"), sem("fill_ok")
        w0_diag, w1_diag, w3_diag = sem("w0_diag"), sem("w1_diag"), sem("w3_diag")
        w0h_ok, w0l_ok, w3h_ok, w3l_ok = sem("w0h_ok"), sem("w0l_ok"), sem("w3h_ok"), sem("w3l_ok")
        tr_full, tr_act, tr_dve = sem("tr_full"), sem("tr_act"), sem("tr_dve")
        a0h_ok, a0l_ok = sem("a0h_ok"), sem("a0l_ok")
        b0h_ok, b0l_ok = sem("b0h_ok"), sem("b0l_ok")
        dn0_full, xr_ok, xrst_ok = sem("dn0_full"), sem("xr_ok"), sem("xrst_ok")
        l0_full, x1h_ok, x1l_ok = sem("l0_full"), sem("x1h_ok"), sem("x1l_ok")
        sign_ok, mix_ok, mh_ok, ml_ok = sem("sign_ok"), sem("mix_ok"), sem("mh_ok"), sem("ml_ok")
        l1_full, x2_ok = sem("l1_full"), sem("x2_ok")
        dn2_full, uwh_ok, uwl_ok = sem("dn2_full"), sem("uwh_ok"), sem("uwl_ok")
        out_full, out_ok = sem("out_full"), sem("out_ok")
        adapt_h, adapt_l = sem("adapt_h"), sem("adapt_l")
        ht_full, ht_ok, g_full, gh_ok, gl_ok = (sem(n) for n in ("ht_full", "ht_ok", "g_full", "gh_ok", "gl_ok"))
        upc_h, upc_l = sem("upc_h"), sem("upc_l")

        USES = [("x", 0), ("x", 1)] + [("w1", c) for c in range(C)] + [("bw", 0), ("x", 2), ("x", 3)]
        for p in range(PAIRS):
            if p == 0:
                USES += [("w3", c) for c in range(C)]
            USES += [("x2", 2 * p), ("x2", 2 * p + 1)]
            if p + 2 < PAIRS:
                USES += [("x", 2 * p + 4), ("x", 2 * p + 5)]
            if p == 0:
                USES += [("b2", 0)]
        BOTH = ("x", "x2", "b2")

        def use(kind, i):
            return USES.index((kind, i))

        def dve_reads(n):
            return sum(k in BOTH for k, _ in USES[:n + 1])

        block = ctx.enter_context(nc.Block())

        def sample_indices(engine, t, last):
            _, regs = nc.values_load_multi_w_load_instructions(
                idx_sb[0:1, t, :], engines=[engine], min_val=0, max_val=last)
            return regs

        @block.sync
        def _(sp):
            def load_x(p):
                if p >= 2:
                    sp.wait_ge(tr_full, use("x", 2 * (p - 2) + 1) + 1)
                sp.dma_start(x_nat[:, p % 2], x[2 * p:2 * p + 2].rearrange("b t d -> t b d")).then_inc(in_x[p % 2], 16)

            def load_mask(b):
                if b >= 2:
                    sp.wait_ge(ml_ok, 2 * (b - 1))
                sp.dma_start(mix[:, b % 2].bitcast(I32), mask[b].rearrange("(c p) o -> p c o", p=P)).then_inc(in_mask[b % 2], 16)

            sp.dma_start(idx_sb[0:1, 0, :], idx0.rearrange("(a n) -> a n", a=1)).then_inc(in_idx0, 16)
            load_x(0)
            for c in range(C):
                sp.dma_start(stage_a[:, c], W0[c * P:(c + 1) * P]).then_inc(in_w0[c], 16)
            sp.dma_start(stage_b[:], W1.rearrange("(q p) i -> p q i", p=P)).then_inc(in_w1, 16)
            sp.wait_ge(in_idx0, 16)
            i0 = sample_indices(mybir.EngineType.SP, 0, A0.shape[0] - 1)
            for b in range(NB):
                sp.dma_start(a0[:, :, b, :], A0[bass.ds(i0[b], 1)].rearrange("a (c p) r -> p (a c) r", p=P)).then_inc(in_a0, 16)
            load_mask(0)
            load_mask(1)
            load_x(1)
            sp.wait_ge(w0l_ok, C)
            sp.dma_start(stage_a[:], W3.rearrange("(q p) i -> p q i", p=P)).then_inc(in_w3, 16)
            sp.wait_ge(in_idx, 32)
            i2 = sample_indices(mybir.EngineType.SP, 1, A2.shape[0] - 1)
            i3 = sample_indices(mybir.EngineType.SP, 2, A3.shape[0] - 1)
            for b in range(NB):
                sp.dma_start(b2[b * R2:(b + 1) * R2, :], B2[bass.ds(i2[b], 1)].rearrange("a r i -> (a r) i")).then_inc(in_b2, 16)
            for b in range(NB):
                sp.dma_start(a3[:, :, b * R3:(b + 1) * R3], A3[bass.ds(i3[b], 1)].rearrange("a (k p) r -> p (a k) r", p=P)).then_inc(in_a3, 16)
            load_mask(2)
            sp.wait_ge(a0l_ok, 2)
            for b in range(NB):
                sp.dma_start(a2[:, :, b * R2:(b + 1) * R2], A2[bass.ds(i2[b], 1)].rearrange("a (k p) r -> p (a k) r", p=P)).then_inc(in_a2, 16)
            load_mask(3)
            for p in range(PAIRS):
                if p + 2 < PAIRS:
                    load_x(p + 2)
                if p + 2 < PAIRS:
                    load_mask(2 * p + 4)
                    load_mask(2 * p + 5)
            for b in (NB - 2, NB - 1):
                sp.wait_ge(out_ok, b + 1)
                sp.dma_start(out[b], stage_b[:, b % C]).then_inc(stored_last, 16)
            for i in range(C):
                sp.wait_ge(stored[i], 16 * len(range(i, NB - 2, C)))
            sp.wait_ge(stored_last, 32)

        @block.gpsimd
        def _(pool):
            pool.memset(ident[:], 0.0).then_inc(zero_ok, 1)
            pool.wait_ge(zero_ok, 1)
            pool.affine_select(out=ident[:], in_=ident[:], compare_op=ALU.not_equal, fill=1.0, base=0,
                               pattern=[[-1, P]], channel_multiplier=1).then_inc(ident_ok, 1)
            pool.wait_ge(in_idx0, 16)
            i0 = sample_indices(mybir.EngineType.Pool, 0, B0.shape[0] - 1)

            def load_b0(p):
                if p >= 1:
                    pool.wait_ge(b0l_ok, p)
                for s in range(2):
                    pool.dma_start(b0[s * HALF:(s + 1) * HALF],
                                   B0[bass.ds(i0[2 * p + s], 1)].to_broadcast([4, R0, D])).then_inc(in_b0, 16)

            load_b0(0)
            pool.memset(f32(xr_st[:]), 0.0).then_inc(const_ok, 1)
            pool.memset(lo_row[:], 0.0).then_inc(const_ok, 1)
            pool.wait_ge(const_ok, 2)
            for s in range(2):
                pool.memset(lo_row[s * HALF + 32:s * HALF + 64], -1.0).then_inc(const_ok, 1)
            pool.wait_ge(in_small, 32)
            pool.wait_ge(const_ok, 4)
            pool.tensor_scalar(c_two[:], c_bc[:], 2.0, None, ALU.mult).then_inc(const_ok, 1)
            pool.tensor_scalar(c_neg[:], c_bc[:], -1.0, None, ALU.mult).then_inc(const_ok, 1)
            load_b0(1)
            pool.wait_ge(in_bw, 16)
            for k in range(4):
                pool.tensor_copy(bw_rep[:, :, k * R3:(k + 1) * R3], bw_nat).then_inc(bw_ok, 1)
            pool.memset(same[:], 1.0).then_inc(zero_ok, 1)
            pool.memset(f32(d_hi[:]), 0.0).then_inc(zero_ok, 1)
            pool.memset(f32(d_lo[:]), 0.0).then_inc(zero_ok, 1)
            pool.memset(f32(up[:]), 0.0).then_inc(zero_ok, 1)
            pool.wait_ge(zero_ok, 5)
            for step, side in enumerate((1, -1)):
                for g in range(2):
                    pool.affine_select(out=same[:, g, :].rearrange("p (b r) -> p b r", r=R2),
                                       in_=same[:, g, :].rearrange("p (b r) -> p b r", r=R2),
                                       compare_op=ALU.is_ge, fill=0.0,
                                       base=side * 4 * g * R3 + (R3 - 1 if side < 0 else 0),
                                       pattern=[[-side * R3, NB], [0, R2]],
                                       channel_multiplier=side).then_inc(fill_ok, 1)
                if step == 0:
                    pool.wait_ge(fill_ok, 2)

            def load_up(p):
                if p >= 1:
                    pool.wait_ge(out_full, 2 * p)
                for s in range(2):
                    b = 2 * p + s
                    for h in range(2):
                        pool.dma_start(f32(up[h * HALF:h * HALF + R2, s]),
                                       f32(g_hl[b * R2:(b + 1) * R2, :, :])).then_inc(in_up, 16)

            load_b0(2)
            pool.wait_ge(gl_ok, 1)
            load_up(0)
            load_b0(3)
            for p in range(1, PAIRS):
                load_up(p)
                for b in (2 * p - 2, 2 * p - 1):
                    pool.wait_ge(out_ok, b + 1)
                    pool.dma_start(out[b], stage_b[:, b % C]).then_inc(stored[b % C], 16)

        @block.scalar
        def _(act):
            for i, t in ((1, idx2), (2, idx3)):
                act.dma_start(idx_sb[0:1, i, :], t.rearrange("(a n) -> a n", a=1)).then_inc(in_idx, 16)
            act.dma_start(c_bc[:], coeff.rearrange("(a n) -> a n", a=1).to_broadcast([P, NB])).then_inc(in_small, 16)
            act.dma_start(bias_bc[:], bias.rearrange("(a n) -> a n", a=1).to_broadcast([P, D])).then_inc(in_small, 16)
            act.dma_start(bw_nat, Bw.rearrange("(q p) r -> p q r", p=P)).then_inc(in_bw, 16)

            def cp(o, i, **kw):
                return nc.scalar.activation(o, i, ACT.Copy, **kw)

            def transposed_hi(kind, b, dst):
                n = use(kind, b)
                act.wait_ge(tr_full, n + 1)
                s = b % 2
                cp(dst[:, :, s * P:(s + 1) * P], p_tr[n % 2][:].rearrange("p (c t) -> p c t", c=C)).then_inc(tr_act, 1)

            def x1_high(p, h):
                act.wait_ge(l0_full, 2 * p + h + 1)
                cp(x1_hi[:, 2 * h:2 * h + 2, :], p_l0[:, 2 * h:2 * h + 2, :]).then_inc(x1h_ok, 1)

            def b0_high(p):
                act.wait_ge(in_b0, 32 * (p + 1))
                if p >= 2:
                    act.wait_ge(l0_full, 2 * (p - 1))
                cp(b0_hi[:, p % 2], b0[:]).then_inc(b0h_ok, 1)

            def xr_high(p):
                act.wait_ge(dn0_full, p + 1)
                if p >= 1:
                    act.wait_ge(xrst_ok, 2 * p)
                cp(xr[:], p_dn[:, 0]).then_inc(xr_ok, 1)

            def sign_times_c(b):
                act.wait_ge(in_mask[b % 2], 16 * (b // 2 + 1))
                for h in range(2):
                    at = mix[:, b % 2, 2 * h:2 * h + 2]
                    nc.scalar.activation(at, at.bitcast(I32), ACT.Identity,
                                         scale=c_two[:, b:b + 1], bias=c_neg[:, b:b + 1]).then_inc(sign_ok, 1)

            def m_high(b, halves=(0, 1)):
                for h in halves:
                    act.wait_ge(mix_ok, 2 * b + h + 1)
                    if b >= 2:
                        act.wait_ge(l1_full, b - 1)
                    at = slice(2 * h, 2 * h + 2)
                    cp(m_hi[:, b % 2, at], mix[:, b % 2, at]).then_inc(mh_ok, 1)

            def uw_high(b):
                s = b % 2
                act.wait_ge(dn2_full, b // 2 + 1)
                rows = slice(s * HALF, (s + 1) * HALF)
                cp(uw_st[rows, s, :], p_dn[rows, 1, s * P:(s + 1) * P]).then_inc(uwh_ok, 1)

            def out_copy(b):
                act.wait_ge(out_full, b + 1)
                if b == 0:
                    act.wait_ge(w3l_ok, 1)
                if b >= C:
                    act.wait_ge(stored[b % C], 16 * (b // C))
                cp(stage_b[:, b % C], p_out[b % 2][:]).then_inc(out_ok, 1)

            def adapters_high():
                act.wait_ge(in_a2, 16 * NB)
                cp(a2_hi[:], a2).then_inc(adapt_h, 1)
                act.wait_ge(in_a3, 16 * NB)
                act.wait_ge(zero_ok, 5)
                cp(d_hi[:, :, :, 32:64].rearrange("p c b r -> p (c b) r"),
                   a3[:].rearrange("p c (b r) -> p (c b) r", r=R3)).then_inc(adapt_h, 1)
                for h in range(2):
                    rows = slice(h * HALF + 32, h * HALF + 64)
                    for s in range(2):
                        cp(up[rows, s, 0], bw_t[rows, :]).then_inc(upc_h, 1)
                n = use("b2", 0)
                act.wait_ge(tr_full, n + 1)
                cp(d_hi[:, :, :, 0:R2].rearrange("p c b r -> p (c b) r"),
                   p_tr[n % 2][:].rearrange("p (c b r) -> p (c b) r", c=C, r=R2)).then_inc(tr_act, 1)
                act.wait_ge(g_full, 1)
                cp(g_hl[:, 0], p_out[0][:]).then_inc(gh_ok, 1)

            transposed_hi("x", 0, xt_hi)
            transposed_hi("x", 1, xt_hi)
            for c in range(C):
                act.wait_ge(w0_diag, c + 1)
                cp(w0_hi[:, c], stage_a[:, c]).then_inc(w0h_ok, 1)
            b0_high(0)
            act.wait_ge(in_a0, 16 * NB)
            for rep in range(2):
                cp(a0_st[:, :, :, rep, 0, :].rearrange("p c b r -> p (c b) r"),
                   a0[:].rearrange("p c b r -> p (c b) r")).then_inc(a0h_ok, 1)
            for c in range(C):
                n = use("w1", c)
                act.wait_ge(tr_full, n + 1)
                cp(w1_t[:, c], p_tr[n % 2][:]).then_inc(tr_act, 1)
            xr_high(0)
            act.wait_ge(tr_full, use("bw", 0) + 1)
            cp(bw_t[:], p_tr[use("bw", 0) % 2][:], scale=0.5).then_inc(tr_act, 1)
            x1_high(0, 0)
            act.wait_ge(const_ok, 6)
            sign_times_c(0)
            m_high(0, [0])
            x1_high(0, 1)
            m_high(0, [1])
            sign_times_c(1)
            transposed_hi("x", 2, xt_hi)
            transposed_hi("x", 3, xt_hi)
            m_high(1)
            b0_high(1)
            for p in range(PAIRS):
                last = p == PAIRS - 1
                if p == 0:
                    for c in range(C):
                        n = use("w3", c)
                        act.wait_ge(tr_full, n + 1)
                        cp(stage_b[:, c], p_tr[n % 2][:]).then_inc(tr_act, 1)
                    xr_high(1)
                    act.wait_ge(w3_diag, C)
                    cp(w3_hi[:], stage_b[:]).then_inc(w3h_ok, 1)
                    x1_high(1, 0)
                    sign_times_c(2)
                    m_high(2)
                    x1_high(1, 1)
                    sign_times_c(3)
                    m_high(3)
                elif not last:
                    b0_high(p + 1)
                    sign_times_c(2 * p + 2)
                    uw_high(2 * p - 2)
                    uw_high(2 * p - 1)
                    m_high(2 * p + 2)
                    xr_high(p + 1)
                    sign_times_c(2 * p + 3)
                    m_high(2 * p + 3)
                    x1_high(p + 1, 0)
                    x1_high(p + 1, 1)
                else:
                    uw_high(2 * p - 2)
                    uw_high(2 * p - 1)
                if p >= 1:
                    out_copy(2 * p - 2)
                    out_copy(2 * p - 1)
                transposed_hi("x2", 2 * p, x2_hi)
                transposed_hi("x2", 2 * p + 1, x2_hi)
                if p + 2 < PAIRS:
                    transposed_hi("x", 2 * p + 4, xt_hi)
                    transposed_hi("x", 2 * p + 5, xt_hi)
                if p == 0:
                    adapters_high()
            uw_high(NB - 2)
            uw_high(NB - 1)
            out_copy(NB - 2)
            out_copy(NB - 1)

        @block.vector
        def _(dve):
            def lo(o, full, hi):
                return nc.vector.tensor_tensor(o, full, f32(hi), ALU.subtract)

            def transposed_lo(kind, b, hi, dst):
                n = use(kind, b)
                dve.wait_ge(tr_act, n + 1)
                cols = slice((b % 2) * P, (b % 2 + 1) * P)
                lo(dst[:, :, cols], p_tr[n % 2][:].rearrange("p (c t) -> p c t", c=C), hi[:, :, cols]).then_inc(tr_dve, 1)

            def x1_low(p, h):
                dve.wait_ge(x1h_ok, 2 * p + h + 1)
                at = slice(2 * h, 2 * h + 2)
                lo(x1_lo[:, at], p_l0[:, at], x1_hi[:, at]).then_inc(x1l_ok, 1)

            def b0_low(p):
                dve.wait_ge(b0h_ok, p + 1)
                lo(b0_lo[:, p % 2], b0[:], b0_hi[:, p % 2]).then_inc(b0l_ok, 1)

            def xr_stack(p):
                dve.wait_ge(xr_ok, p + 1)
                for s in range(2):
                    rows, cols = slice(s * HALF, (s + 1) * HALF), slice(s * P, (s + 1) * P)
                    nc.vector.scalar_tensor_tensor(xr_st[rows, cols], f32(xr[rows, cols]), lo_row[rows, 0:1],
                                                   p_dn[rows, 0, cols], ALU.mult, ALU.add).then_inc(xrst_ok, 1)

            def mix_weights(b):
                for h in range(2):
                    dve.wait_ge(sign_ok, 2 * b + h + 1)
                    at = slice(2 * h, 2 * h + 2)
                    nc.vector.tensor_tensor(mix[:, b % 2, at], mix[:, b % 2, at], w1_t[:, at], ALU.add).then_inc(mix_ok, 1)

            def m_low(b, halves=(0, 1)):
                for h in halves:
                    dve.wait_ge(mh_ok, 2 * b + h + 1)
                    at = slice(2 * h, 2 * h + 2)
                    lo(m_lo[:, b % 2, at], mix[:, b % 2, at], m_hi[:, b % 2, at]).then_inc(ml_ok, 1)

            def add_identity(t, c, done):
                at = t[:, c, c * P:(c + 1) * P]
                nc.vector.tensor_tensor(at, at, ident[:], ALU.add).then_inc(done, 1)

            def x2_bias(b):
                dve.wait_ge(l1_full, b + 1)
                nc.vector.tensor_tensor(x2_nat[:, b % 2], p_l1[:], bias_bc[:], ALU.add).then_inc(x2_ok, 1)

            def uw_low(b):
                s = b % 2
                dve.wait_ge(uwh_ok, b + 1)
                rows, other = slice(s * HALF, (s + 1) * HALF), slice((1 - s) * HALF, (2 - s) * HALF)
                lo(uw_st[other, s, :], p_dn[rows, 1, s * P:(s + 1) * P], uw_st[rows, s, :]).then_inc(uwl_ok, 1)

            def adapters_low():
                dve.wait_ge(adapt_h, 1)
                lo(a2_lo[:], a2, a2_hi[:]).then_inc(adapt_l, 1)
                dve.wait_ge(adapt_h, 2)
                lo(d_lo[:, :, :, 32:64].rearrange("p c b r -> p (c b) r"),
                   a3[:].rearrange("p c (b r) -> p (c b) r", r=R3),
                   d_hi[:, :, :, 32:64].rearrange("p c b r -> p (c b) r")).then_inc(adapt_l, 1)
                for h in range(2):
                    rows = slice(h * HALF + 32, h * HALF + 64)
                    for s in range(2):
                        dve.wait_ge(upc_h, 2 * h + s + 1)
                        lo(up[rows, s, 1], bw_t[rows, :], up[rows, s, 0]).then_inc(upc_l, 1)
                n = use("b2", 0)
                dve.wait_ge(tr_act, n + 1)
                lo(d_lo[:, :, :, 0:R2].rearrange("p c b r -> p (c b) r"),
                   p_tr[n % 2][:].rearrange("p (c b r) -> p (c b) r", c=C, r=R2),
                   d_hi[:, :, :, 0:R2].rearrange("p c b r -> p (c b) r")).then_inc(tr_dve, 1)
                dve.wait_ge(ht_full, 1)
                dve.wait_ge(fill_ok, 4)
                nc.vector.tensor_tensor(h_t[:].rearrange("p g n -> p (g n)"), p_out[1][:, 0:2 * P],
                                        same[:].rearrange("p g n -> p (g n)"), ALU.mult).then_inc(ht_ok, 1)
                dve.wait_ge(gh_ok, 1)
                lo(g_hl[:, 1], p_out[0][:], g_hl[:, 0]).then_inc(gl_ok, 1)

            def w0_low(c):
                dve.wait_ge(w0h_ok, c + 1)
                lo(w0_lo[:, c], stage_a[:, c], w0_hi[:, c]).then_inc(w0l_ok, 1)

            dve.wait_ge(ident_ok, 1)
            transposed_lo("x", 0, xt_hi, xt_lo)
            transposed_lo("x", 1, xt_hi, xt_lo)
            for c in range(C):
                dve.wait_ge(in_w0[c], 16)
                add_identity(stage_a, c, w0_diag)
                if c >= 1:
                    w0_low(c - 1)
            w0_low(C - 1)
            b0_low(0)
            for rep in range(2):
                dve.wait_ge(a0h_ok, rep + 1)
                lo(a0_st[:, :, :, rep, 1, :].rearrange("p c b r -> p (c b) r"),
                   a0[:].rearrange("p c b r -> p (c b) r"),
                   a0_st[:, :, :, rep, 0, :].rearrange("p c b r -> p (c b) r")).then_inc(a0l_ok, 1)
            for c in range(C):
                dve.wait_ge(tr_act, use("w1", c) + 1)
                add_identity(w1_t, c, w1_diag)
            dve.wait_ge(const_ok, 4)
            xr_stack(0)
            x1_low(0, 0)
            dve.wait_ge(w1_diag, C)
            mix_weights(0)
            m_low(0, [0])
            x1_low(0, 1)
            m_low(0, [1])
            mix_weights(1)
            transposed_lo("x", 2, xt_hi, xt_lo)
            transposed_lo("x", 3, xt_hi, xt_lo)
            m_low(1, [0])
            dve.wait_ge(in_small, 32)
            x2_bias(0)
            m_low(1, [1])
            b0_low(1)
            for p in range(PAIRS):
                last = p == PAIRS - 1
                if p == 0:
                    x2_bias(1)
                    for c in range(C):
                        dve.wait_ge(tr_act, use("w3", c) + 1)
                        add_identity(stage_b, c, w3_diag)
                    xr_stack(1)
                    dve.wait_ge(w3h_ok, 1)
                    lo(w3_lo[:], stage_b[:], w3_hi[:]).then_inc(w3l_ok, 1)
                    x1_low(1, 0)
                    mix_weights(2)
                    m_low(2)
                    x1_low(1, 1)
                    mix_weights(3)
                    m_low(3)
                elif not last:
                    b0_low(p + 1)
                    x2_bias(2 * p)
                    mix_weights(2 * p + 2)
                    uw_low(2 * p - 2)
                    uw_low(2 * p - 1)
                    x2_bias(2 * p + 1)
                    xr_stack(p + 1)
                    m_low(2 * p + 2)
                    mix_weights(2 * p + 3)
                    m_low(2 * p + 3)
                    x1_low(p + 1, 0)
                    x1_low(p + 1, 1)
                else:
                    x2_bias(2 * p)
                    uw_low(2 * p - 2)
                    uw_low(2 * p - 1)
                    x2_bias(2 * p + 1)
                transposed_lo("x2", 2 * p, x2_hi, x2_lo)
                transposed_lo("x2", 2 * p + 1, x2_hi, x2_lo)
                if p + 2 < PAIRS:
                    transposed_lo("x", 2 * p + 4, xt_hi, xt_lo)
                    transposed_lo("x", 2 * p + 5, xt_hi, xt_lo)
                if p == 0:
                    adapters_low()
            uw_low(NB - 2)
            uw_low(NB - 1)

        @block.tensor
        def _(pe):
            mm = nc.tensor.matmul

            def bank_free(n):
                if n >= 2:
                    pe.wait_ge(tr_act, n - 1)
                    if dve_reads(n - 2):
                        pe.wait_ge(tr_dve, dve_reads(n - 2))

            def transpose4(kind, i, blocks):
                n = use(kind, i)
                bank_free(n)
                for c in range(C):
                    t = nc.tensor.transpose(p_tr[n % 2][:, c * P:(c + 1) * P], blocks(c), ident[:])
                t.then_inc(tr_full, 1)

            def transpose_x(b):
                pe.wait_ge(in_x[b // 2 % 2], 16 * (b // 4 + 1))
                transpose4("x", b, lambda c: x_nat[:, b // 2 % 2, b % 2, c * P:(c + 1) * P])

            def transpose_x2(b):
                pe.wait_ge(x2_ok, b + 1)
                transpose4("x2", b, lambda c: x2_nat[:, b % 2, c * P:(c + 1) * P])

            def down0(p):
                pe.wait_ge(tr_act, use("x", 2 * p + 1) + 1)
                pe.wait_ge(tr_dve, dve_reads(use("x", 2 * p + 1)))
                if p == 0:
                    pe.wait_ge(a0l_ok, 2)
                else:
                    pe.wait_ge(xrst_ok, 2 * p)
                if p >= 2:
                    pe.wait_ge(uwl_ok, 2 * (p - 1))
                for c in range(C):
                    w = a0_st[:, c, 2 * p:2 * p + 2].rearrange("p b e h r -> p (b e h r)")
                    mm(p_dn[:, 0], w, xt_hi[:, c], start=(c == 0), stop=False)
                    t = mm(p_dn[:, 0], w, xt_lo[:, c], start=False, stop=(c == C - 1))
                t.then_inc(dn0_full, 1)

            def layer0(p, between=lambda: None):
                if p >= 1:
                    pe.wait_ge(x1l_ok, 2 * p)
                for q in range(C):
                    o = slice(q * P, (q + 1) * P)
                    for c in range(C):
                        if p == 0 and q == 0:
                            pe.wait_ge(w0l_ok, c + 1)
                        mm(p_l0[:, q], w0_hi[:, c, o], xt_hi[:, c], start=(c == 0), stop=False)
                        mm(p_l0[:, q], w0_hi[:, c, o], xt_lo[:, c], start=False, stop=False)
                        mm(p_l0[:, q], w0_lo[:, c, o], xt_hi[:, c], start=False, stop=False)
                    if q == 0:
                        between()
                        pe.wait_ge(xrst_ok, 2 * p + 2)
                        pe.wait_ge(b0l_ok, p + 1)
                    mm(p_l0[:, q], b0_hi[:, p % 2, o], xr_st[:], start=False, stop=False)
                    t = mm(p_l0[:, q], b0_lo[:, p % 2, o], xr_st[:], start=False, stop=True)
                    if q % 2:
                        t.then_inc(l0_full, 1)

            def layer1(b):
                pe.wait_ge(x1l_ok, 2 * (b // 2) + 2)
                if b >= 1:
                    pe.wait_ge(x2_ok, b)
                tok = slice((b % 2) * P, (b % 2 + 1) * P)
                for c in range(C):
                    if c % 2 == 0:
                        pe.wait_ge(ml_ok, 2 * b + c // 2 + 1)
                    mm(p_l1[:], x1_hi[:, c, tok], m_hi[:, b % 2, c], start=(c == 0), stop=False)
                    mm(p_l1[:], x1_hi[:, c, tok], m_lo[:, b % 2, c], start=False, stop=False)
                    t = mm(p_l1[:], x1_lo[:, c, tok], m_hi[:, b % 2, c], start=False, stop=(c == C - 1))
                t.then_inc(l1_full, 1)

            def down2(p):
                pe.wait_ge(tr_act, use("x2", 2 * p + 1) + 1)
                pe.wait_ge(tr_dve, dve_reads(use("x2", 2 * p + 1)))
                if p == 0:
                    pe.wait_ge(tr_dve, dve_reads(use("b2", 0)))
                    pe.wait_ge(adapt_l, 2)
                else:
                    pe.wait_ge(uwl_ok, 2 * p)
                pe.wait_ge(xrst_ok, 2 * min(p + 2, PAIRS))
                for c in range(C):
                    wh = d_hi[:, c, 2 * p:2 * p + 2].rearrange("p b r -> p (b r)")
                    wl = d_lo[:, c, 2 * p:2 * p + 2].rearrange("p b r -> p (b r)")
                    mm(p_dn[:, 1], wh, x2_hi[:, c], start=(c == 0), stop=False)
                    mm(p_dn[:, 1], wh, x2_lo[:, c], start=False, stop=False)
                    t = mm(p_dn[:, 1], wl, x2_hi[:, c], start=False, stop=(c == C - 1))
                t.then_inc(dn2_full, 1)

            def layer23(b):
                s = b % 2
                tok = slice(s * P, (s + 1) * P)
                po = p_out[b % 2]
                if b == 0:
                    pe.wait_ge(w3l_ok, 1)
                    pe.wait_ge(gl_ok, 1)
                if b >= 2:
                    pe.wait_ge(out_ok, b - 1)
                for c in range(C):
                    mm(po[:], x2_hi[:, c, tok], w3_hi[:, c], start=(c == 0), stop=False)
                    mm(po[:], x2_hi[:, c, tok], w3_lo[:, c], start=False, stop=False)
                    mm(po[:], x2_lo[:, c, tok], w3_hi[:, c], start=False, stop=False)
                pe.wait_ge(uwl_ok, b + 1)
                pe.wait_ge(in_up, 64 * (b // 2 + 1))
                if b == 0:
                    pe.wait_ge(upc_l, 4)
                mm(po[:], uw_st[:, s], up[:, s, 0], start=False, stop=False)
                mm(po[:], uw_st[:, s], up[:, s, 1], start=False, stop=True).then_inc(out_full, 1)

            def adapters():
                pe.wait_ge(in_b2, 16 * NB)
                transpose4("b2", 0, lambda c: b2[:, c * P:(c + 1) * P])
                pe.wait_ge(in_a2, 16 * NB)
                pe.wait_ge(in_a3, 16 * NB)
                for g in range(2):
                    for k in range(C):
                        t = mm(p_out[1][:, g * P:(g + 1) * P], a3[:, k, g * P:(g + 1) * P], a2[:, k, :],
                               start=(k == 0), stop=(k == C - 1))
                t.then_inc(ht_full, 1)
                pe.wait_ge(adapt_l, 1)
                pe.wait_ge(w3l_ok, 1)
                for k in range(C):
                    mm(p_out[0][:], a2_hi[:, k], w3_hi[:, k], start=(k == 0), stop=False)
                    mm(p_out[0][:], a2_hi[:, k], w3_lo[:, k], start=False, stop=False)
                    mm(p_out[0][:], a2_lo[:, k], w3_hi[:, k], start=False, stop=False)
                pe.wait_ge(ht_ok, 1)
                for g in range(2):
                    t = mm(p_out[0][:], h_t[:, g], bw_t[:], start=False, stop=(g == 1))
                t.then_inc(g_full, 1)

            pe.wait_ge(ident_ok, 1)
            transpose_x(0)
            transpose_x(1)

            def first_side_path():
                pe.wait_ge(in_w1, 16)
                for i in range(C):
                    transpose4("w1", i, lambda q: stage_b[:, q, i * P:(i + 1) * P])
                down0(0)
                pe.wait_ge(bw_ok, 4)
                transpose4("bw", 0, lambda c: bw_rep[:, c, :])

            layer0(0, first_side_path)
            for p in range(PAIRS):
                layer1(2 * p)
                if p == 0:
                    transpose_x(2)
                    transpose_x(3)
                else:
                    down2(p - 1)
                layer1(2 * p + 1)
                if p == 0:
                    pe.wait_ge(in_w3, 16)
                    for i in range(C):
                        transpose4("w3", i, lambda q: stage_a[:, q, i * P:(i + 1) * P])
                if p + 1 < PAIRS:
                    down0(p + 1)
                    layer0(p + 1)
                if p >= 1:
                    layer23(2 * p - 2)
                    layer23(2 * p - 1)
                transpose_x2(2 * p)
                transpose_x2(2 * p + 1)
                if p + 2 < PAIRS:
                    transpose_x(2 * p + 4)
                    transpose_x(2 * p + 5)
                if p == 0:
                    adapters()
            down2(PAIRS - 1)
            layer23(NB - 2)
            layer23(NB - 1)


_INS = ["x", "itok_B_0_15", "condB_coeff", "itok_B_3_7", "itok_B_0_2", "mask_Bx4096x4096_ik1",
        "L0_cond_W", "L0_cond_lora_A", "L0_cond_lora_B", "L1_cond_W", "L1_cond_b",
        "L2_cond_A", "L2_cond_B", "L3_cond_W", "L3_cond_lora_A", "L3_cond_lora_B_w"]


def kernel(**inputs):
    import numpy as _np
    import concourse.bacc as _bacc
    from concourse import mybir as _mybir
    from concourse.bass_utils import run_bass_kernel_spmd as _run

    nc = _bacc.Bacc("TRN2", target_bir_lowering=False, num_devices=1)
    arrays, args = {}, []
    for name in _INS:
        a = _np.ascontiguousarray(inputs[name])
        arrays[f"in_{name}_dram"] = a
        args.append(nc.dram_tensor(f"in_{name}_dram", a.shape, _mybir.dt.from_np(a.dtype), kind="ExternalInput").ap())
    shape = inputs["x"].shape
    args.append(nc.dram_tensor("out_0_dram", shape, _mybir.dt.float32, kind="ExternalOutput").ap())
    build(nc, *args)
    r = _run(nc, [arrays], core_ids=[0])
    return r.results[0]["out_0_dram"]
```

```python
from contextlib import ExitStack

import concourse.bass as bass
from concourse import mybir

F32 = mybir.dt.float32
F32R = mybir.dt.float32r
I32 = mybir.dt.int32
ALU = mybir.AluOpType
ACT = mybir.ActivationFunctionType


def build(nc, x, idx0, coeff, idx2, idx3, mask, W0, A0, B0, W1, bias, A2, B2, W3, A3, Bw, out):
    P = 128
    NB, S, D = x.shape
    C = D // P
    PAIRS = NB // 2
    R0 = A0.shape[2]
    R2 = A2.shape[2]
    R3 = A3.shape[2]
    HALF = P // 2
    assert S == P and R0 == 16 and R2 == 16 and R3 == 32 and NB * R2 == P

    ctx = ExitStack()
    with ctx:
        def sb(name, shape, dt=F32):
            return ctx.enter_context(nc.sbuf_tensor(name, shape, dt))

        def ps(name, shape):
            return ctx.enter_context(nc.psum_tensor(name, shape, F32))

        def sem(name):
            return ctx.enter_context(nc.semaphore(name))

        def f32(ap):
            return ap.bitcast(F32)

        x_nat = sb("x_nat", [P, 2, 2, D])
        stage_a = sb("stage_a", [P, C, D])
        stage_b = sb("stage_b", [P, C, D])
        w0_hi, w0_lo = sb("w0_hi", [P, C, D], F32R), sb("w0_lo", [P, C, D], F32R)
        w1_t = sb("w1_t", [P, C, D])
        w3_hi, w3_lo = sb("w3_hi", [P, C, D], F32R), sb("w3_lo", [P, C, D], F32R)
        xt_hi, xt_lo = sb("xt_hi", [P, C, 2 * P], F32R), sb("xt_lo", [P, C, 2 * P], F32R)
        pair_a = sb("pair_a_hi", [P, C, 2 * P], F32R), sb("pair_a_lo", [P, C, 2 * P], F32R)
        pair_b = sb("pair_b_hi", [P, C, 2 * P], F32R), sb("pair_b_lo", [P, C, 2 * P], F32R)

        def x1_of(p):
            return pair_b if p == 0 else pair_a

        def xt_of(p):
            if p == 1:
                return m_hi[:, 1, :, 0:2 * P], m_lo[:, 1, :, 0:2 * P]
            return xt_hi[:], xt_lo[:]

        def b0_of(p):
            return f32(g_hl[:, 0]) if p == 1 else b0[:]

        def x2_of(p):
            return pair_a if p == PAIRS - 1 else pair_b

        x2_nat = sb("x2_nat", [P, 2, D])
        mix = sb("mix", [P, 2, C, D])
        m_hi, m_lo = sb("m_hi", [P, 2, C, D], F32R), sb("m_lo", [P, 2, C, D], F32R)
        a0 = sb("a0", [P, C, NB, R0])
        b2 = sb("b2", [P, D])
        a3 = sb("a3", [P, C, NB * R3])
        a0_st = sb("a0_st", [P, C, NB, 2, 2, R0], F32R)
        b0 = sb("b0", [P, D])
        b0_hi, b0_lo = sb("b0_hi", [P, 2, D], F32R), sb("b0_lo", [P, 2, D], F32R)
        xr = sb("xr", [P, 2 * P], F32R)
        xr_st = sb("xr_st", [P, 2 * P], F32R)
        a2_hi, a2_lo = sb("a2_hi", [P, C, P], F32R), sb("a2_lo", [P, C, P], F32R)
        d_hi, d_lo = sb("d_hi", [P, C, NB, HALF], F32R), sb("d_lo", [P, C, NB, HALF], F32R)
        uw_st = sb("uw_st", [P, 2, P], F32R)
        bw_t = sb("bw_t", [P, D])
        h_t = sb("h_t", [P, 2, P])
        same = sb("same", [P, HALF])
        g_hl = sb("g_hl", [P, 2, D], F32R)
        up = sb("up", [P, 2, 2, D], F32R)
        ident_r = sb("ident", [P, P], F32R)
        ident = f32(ident_r[:])
        bias_bc = sb("bias_bc", [P, D])
        c_bc = sb("c_bc", [P, NB])
        c_two = sb("c_two", [P, NB])
        c_neg = sb("c_neg", [P, NB])
        lo_row = sb("lo_row", [P, 1])
        idx_sb = sb("idx_sb", [1, 3, NB], I32)

        a2 = a0[:].rearrange("p c b r -> p c (b r)")
        bw_nat = x2_nat[:, 1, 0:C * R3].rearrange("p (q r) -> p q r", q=C)
        bw_rep = x2_nat[:, 0, :].rearrange("p (q n) -> p q n", q=C)

        p_tr = [ps(f"p_tr{i}", [P, D]) for i in range(2)]
        p_l0 = ps("p_l0", [P, C, 2 * P])
        p_l1 = ps("p_l1", [P, D])
        p_dn = ps("p_dn", [P, 2, 2 * P])
        p_out = [ps(f"p_out{i}", [P, D]) for i in range(2)]

        in_idx0, in_idx, bw_ok = sem("in_idx0"), sem("in_idx"), sem("bw_ok")
        in_coeff, in_bias, in_bw = sem("in_coeff"), sem("in_bias"), sem("in_bw")
        in_x_first, in_x = sem("in_x_first"), [sem(f"in_x{i}") for i in range(2)]
        in_w0 = [sem(f"in_w0{q}") for q in range(C)]
        in_w1, in_w3 = sem("in_w1"), sem("in_w3")
        in_mask = [sem(f"in_mask{i}") for i in range(2)]
        in_a0_first, in_a0 = sem("in_a0_first"), sem("in_a0")
        in_b0 = [sem(f"in_b0{i}") for i in range(2)]
        in_up = [sem(f"in_up{s}") for s in range(2)]
        in_a2, in_b2, in_a3, in_upc = (sem(n) for n in ("in_a2", "in_b2", "in_a3", "in_upc"))
        stored = [sem(f"stored{i}") for i in range(C)]
        stored_last = sem("stored_last")
        ident_ok, const_ok, zero_ok, fill_ok = sem("ident_ok"), sem("const_ok"), sem("zero_ok"), sem("fill_ok")
        w0_diag, w1_diag, w0h_ok, w0l_ok = sem("w0_diag"), sem("w1_diag"), sem("w0h_ok"), sem("w0l_ok")
        tr_full, tr_act, tr_dve = sem("tr_full"), sem("tr_act"), sem("tr_dve")
        a0h_ok, a0l_ok = sem("a0h_ok"), sem("a0l_ok")
        b0h_ok, b0l_ok = sem("b0h_ok"), sem("b0l_ok")
        dn0_full, xr_ok, xrst_ok = sem("dn0_full"), sem("xr_ok"), sem("xrst_ok")
        l0_full, x1h_ok, x1l_ok = sem("l0_full"), sem("x1h_ok"), sem("x1l_ok")
        mix_ok, mh_ok, ml_ok = sem("mix_ok"), sem("mh_ok"), sem("ml_ok")
        l1_full, x2_ok = sem("l1_full"), sem("x2_ok")
        dn2_full, uwh_ok, uwl_ok = sem("dn2_full"), sem("uwh_ok"), sem("uwl_ok")
        out_full, out_ok = sem("out_full"), sem("out_ok")
        a2h_ok, a2l_ok, a3h_ok, a3l_ok = sem("a2h_ok"), sem("a2l_ok"), sem("a3h_ok"), sem("a3l_ok")
        ht_full, ht_ok, g_full, gh_ok, gl_ok = (sem(n) for n in ("ht_full", "ht_ok", "g_full", "gh_ok", "gl_ok"))
        upc_h, upc_l = sem("upc_h"), sem("upc_l")

        USES = [("x", b) for b in range(4)] + [("w1", c) for c in range(C)]
        USES += [("w3", 0), ("w3", 1), ("bw", 0), ("w3", 2), ("w3", 3), ("b2", 0)]
        USES += [("x2", 0), ("x", 4), ("x", 5), ("x2", 1)]
        for p in range(1, PAIRS):
            if p + 2 < PAIRS:
                USES += [("x", 2 * p + 4), ("x", 2 * p + 5)]
            USES += [("x2", 2 * p), ("x2", 2 * p + 1)]
        BOTH = ("x", "x2", "b2", "w3")

        FIRST = (0, 2, 1, 3)

        def use(kind, i):
            return USES.index((kind, i))

        def dve_reads(n):
            return sum(k in BOTH for k, _ in USES[:n + 1])

        block = ctx.enter_context(nc.Block())

        def sample_indices(engine, t, last):
            _, regs = nc.values_load_multi_w_load_instructions(
                idx_sb[0:1, t, :], engines=[engine], min_val=0, max_val=last)
            return regs

        @block.sync
        def _(sp):
            def load_x(p):
                if p >= 2:
                    sp.wait_ge(tr_full, use("x", 2 * (p - 2) + 1) + 1)
                sp.dma_start(x_nat[:, p % 2], x[2 * p:2 * p + 2].rearrange("b t d -> t b d")).then_inc(in_x[p % 2], 16)

            def load_mask(b):
                if b >= 2:
                    sp.wait_ge(ml_ok, 2 * (b - 1))
                sp.dma_start(mix[:, b % 2].bitcast(I32), mask[b].rearrange("(c p) o -> p c o", p=P)).then_inc(in_mask[b % 2], 16)

            sp.dma_start(x_nat[:, 0, 0], x[0]).then_inc(in_x_first, 16)
            sp.dma_start(idx_sb[0:1, 0, :], idx0.rearrange("(a n) -> a n", a=1)).then_inc(in_idx0, 16)
            sp.dma_start(x_nat[:, 0, 1], x[1]).then_inc(in_x[0], 16)
            for q in FIRST:
                o = slice(q * P, (q + 1) * P)
                sp.dma_start(stage_a[:, :, o], W0.rearrange("(c p) o -> p c o", p=P)[:, :, o]).then_inc(in_w0[q], 16)
            load_x(1)
            sp.dma_start(c_bc[:], coeff.rearrange("(a n) -> a n", a=1).to_broadcast([P, NB])).then_inc(in_coeff, 16)
            for i, t in ((1, idx2), (2, idx3)):
                sp.dma_start(idx_sb[0:1, i, :], t.rearrange("(a n) -> a n", a=1)).then_inc(in_idx, 16)
            sp.wait_ge(in_idx0, 16)
            i0 = sample_indices(mybir.EngineType.SP, 0, A0.shape[0] - 1)

            def load_a0(b, done):
                sp.dma_start(a0[:, :, b, :], A0[bass.ds(i0[b], 1)].rearrange("a (c p) r -> p (a c) r", p=P)).then_inc(done, 16)

            load_a0(0, in_a0_first)
            load_a0(1, in_a0_first)
            sp.dma_start(stage_b[:], W1.rearrange("(q p) i -> p q i", p=P)).then_inc(in_w1, 16)
            for b in range(2, NB):
                load_a0(b, in_a0)
            load_mask(0)
            sp.dma_start(bw_nat, Bw.rearrange("(q p) r -> p q r", p=P)).then_inc(in_bw, 16)
            sp.wait_ge(w0l_ok, C)
            sp.dma_start(stage_a[:], W3.rearrange("(q p) i -> p q i", p=P)).then_inc(in_w3, 16)
            load_mask(1)
            sp.dma_start(bias_bc[:], bias.rearrange("(a n) -> a n", a=1).to_broadcast([P, D])).then_inc(in_bias, 16)
            sp.wait_ge(in_idx, 32)
            i2 = sample_indices(mybir.EngineType.SP, 1, A2.shape[0] - 1)
            for b in range(NB):
                sp.dma_start(b2[b * R2:(b + 1) * R2, :], B2[bass.ds(i2[b], 1)].rearrange("a r i -> (a r) i")).then_inc(in_b2, 16)
            sp.wait_ge(a0l_ok, 4)
            for b in range(NB):
                sp.dma_start(a2[:, :, b * R2:(b + 1) * R2], A2[bass.ds(i2[b], 1)].rearrange("a (k p) r -> p (a k) r", p=P)).then_inc(in_a2, 16)
            load_mask(2)
            load_x(2)
            load_mask(3)
            load_x(3)

            def load_up(b):
                if b >= 2:
                    sp.wait_ge(out_full, b - 1)
                for h in range(2):
                    sp.dma_start(f32(up[h * HALF:h * HALF + R2, b % 2]),
                                 f32(g_hl[b * R2:(b + 1) * R2, :, :])).then_inc(in_up[b % 2], 16)

            load_mask(4)
            sp.wait_ge(gl_ok, 1)
            sp.wait_ge(zero_ok, 6)
            load_up(0)
            load_up(1)
            for b in range(5, NB):
                load_mask(b)
            for b in range(2, NB):
                load_up(b)
            sp.wait_ge(out_ok, NB - 1)
            sp.dma_start(out[NB - 2], stage_b[:, (NB - 2) % C]).then_inc(stored_last, 16)
            for h in range(2):
                sp.wait_ge(out_ok, NB + h)
                cols = slice(h * D // 2, (h + 1) * D // 2)
                sp.dma_start(out[NB - 1][:, cols], stage_b[:, (NB - 1) % C, cols]).then_inc(stored_last, 16)
            for i in range(C):
                sp.wait_ge(stored[i], 16 * len(range(i, NB - 2, C)))
            sp.wait_ge(stored_last, 48)

        @block.gpsimd
        def _(pool):
            pool.memset(ident, 0.0).then_inc(zero_ok, 1)
            pool.wait_ge(zero_ok, 1)
            pool.affine_select(out=ident_r[:], in_=ident, compare_op=ALU.not_equal, fill=1.0, base=0,
                               pattern=[[-1, P]], channel_multiplier=1).then_inc(ident_ok, 1)
            pool.wait_ge(in_idx0, 16)
            i0 = sample_indices(mybir.EngineType.Pool, 0, B0.shape[0] - 1)

            def load_b0(p):
                if p >= 2:
                    pool.wait_ge(b0l_ok, 1 if p == 2 else p)
                for s in range(2):
                    pool.dma_start(b0_of(p)[s * HALF:(s + 1) * HALF],
                                   B0[bass.ds(i0[2 * p + s], 1)].to_broadcast([4, R0, D])).then_inc(in_b0[p % 2], 16)

            load_b0(0)
            load_b0(1)
            pool.memset(f32(xr_st[:]), 0.0).then_inc(const_ok, 1)
            pool.memset(lo_row[:], 0.0).then_inc(const_ok, 1)
            pool.wait_ge(const_ok, 2)
            for s in range(2):
                pool.memset(lo_row[s * HALF + 32:s * HALF + 64], -1.0).then_inc(const_ok, 1)
            pool.wait_ge(const_ok, 4)
            pool.memset(same[:], 1.0).then_inc(zero_ok, 1)
            pool.memset(h_t[:], 0.0).then_inc(zero_ok, 1)
            pool.memset(f32(d_hi[:]), 0.0).then_inc(zero_ok, 1)
            pool.memset(f32(d_lo[:]), 0.0).then_inc(zero_ok, 1)
            pool.wait_ge(in_coeff, 16)
            pool.tensor_scalar(c_two[:], c_bc[:], 2.0, None, ALU.mult).then_inc(const_ok, 1)
            pool.tensor_scalar(c_neg[:], c_bc[:], -1.0, None, ALU.mult).then_inc(const_ok, 1)
            pool.memset(f32(up[:]), 0.0).then_inc(zero_ok, 1)
            pool.wait_ge(in_idx, 32)
            i3 = sample_indices(mybir.EngineType.Pool, 2, A3.shape[0] - 1)
            for b in range(NB):
                pool.dma_start(a3[:, :, b * R3:(b + 1) * R3], A3[bass.ds(i3[b], 1)].rearrange("a (k p) r -> p (a k) r", p=P)).then_inc(in_a3, 16)
            pool.wait_ge(in_bw, 16)
            for k in range(4):
                pool.tensor_copy(bw_rep[:, :, k * R3:(k + 1) * R3], bw_nat).then_inc(bw_ok, 1)
            pool.wait_ge(zero_ok, 6)
            for side in (1, -1):
                pool.affine_select(out=same[:].rearrange("p (b r) -> p b r", r=R2),
                                   in_=same[:].rearrange("p (b r) -> p b r", r=R2),
                                   compare_op=ALU.is_ge, fill=0.0, base=(R3 - 1 if side < 0 else 0),
                                   pattern=[[-side * R3, 4], [0, R2]], channel_multiplier=side).then_inc(fill_ok, 1)
                if side > 0:
                    pool.wait_ge(fill_ok, 1)
            load_b0(2)
            load_b0(3)
            for b in range(NB - 2):
                pool.wait_ge(out_ok, b + 1)
                pool.dma_start(out[b], stage_b[:, b % C]).then_inc(stored[b % C], 16)

        @block.scalar
        def _(act):
            def cp(o, i, **kw):
                return nc.scalar.activation(o, i, ACT.Copy, **kw)

            def transposed_hi(kind, b, dst):
                n = use(kind, b)
                act.wait_ge(tr_full, n + 1)
                s = b % 2
                cp(dst[:, :, s * P:(s + 1) * P], p_tr[n % 2][:].rearrange("p (c t) -> p c t", c=C)).then_inc(tr_act, 1)

            def x1_high(p, h):
                act.wait_ge(l0_full, 2 * p + h + 1)
                if p >= 2:
                    act.wait_ge(l1_full, 2 * p)
                cp(x1_of(p)[0][:, 2 * h:2 * h + 2, :], p_l0[:, 2 * h:2 * h + 2, :]).then_inc(x1h_ok, 1)

            def b0_high(p):
                act.wait_ge(in_b0[p % 2], 32 * (p // 2 + 1))
                if p >= 2:
                    act.wait_ge(l0_full, 2 * (p - 1))
                cp(b0_hi[:, p % 2], b0_of(p)).then_inc(b0h_ok, 1)

            def a0_high(b, n):
                for rep in range(2):
                    cp(a0_st[:, :, b:b + n, rep, 0, :], a0[:, :, b:b + n, :]).then_inc(a0h_ok, 1)

            def xr_high(p):
                act.wait_ge(dn0_full, p + 1)
                if p >= 1:
                    act.wait_ge(xrst_ok, 2 * p)
                cp(xr[:], p_dn[:, 0]).then_inc(xr_ok, 1)

            def m_high(b, halves=(0, 1)):
                for h in halves:
                    act.wait_ge(mix_ok, 2 * b + h + 1)
                    if b == 1:
                        act.wait_ge(l0_full, 4)
                    if b >= 2:
                        act.wait_ge(l1_full, b - 1)
                    at = slice(2 * h, 2 * h + 2)
                    nc.scalar.activation(m_hi[:, b % 2, at], mix[:, b % 2, at], ACT.Identity,
                                         bias=c_neg[:, b:b + 1]).then_inc(mh_ok, 1)

            def uw_high(b):
                s = b % 2
                act.wait_ge(dn2_full, b // 2 + 1)
                rows = slice(s * HALF, (s + 1) * HALF)
                cp(uw_st[rows, s, :], p_dn[rows, 1, s * P:(s + 1) * P]).then_inc(uwh_ok, 1)

            def out_copy(b):
                act.wait_ge(out_full, b + 1)
                if b >= C:
                    act.wait_ge(stored[b % C], 16 * (b // C))
                cp(stage_b[:, b % C], p_out[b % 2][:]).then_inc(out_ok, 1)

            def a2_high():
                act.wait_ge(in_a2, 16 * NB)
                cp(a2_hi[:], a2).then_inc(a2h_ok, 1)

            def b2_high():
                act.wait_ge(zero_ok, 6)
                n = use("b2", 0)
                act.wait_ge(tr_full, n + 1)
                cp(d_hi[:, :, :, 0:R2].rearrange("p c b r -> p (c b) r"),
                   p_tr[n % 2][:].rearrange("p (c b r) -> p (c b) r", c=C, r=R2)).then_inc(tr_act, 1)

            def a3_high():
                act.wait_ge(in_a3, 16 * NB)
                cp(d_hi[:, :, :, 32:64].rearrange("p c b r -> p (c b) r"),
                   a3[:].rearrange("p c (b r) -> p (c b) r", r=R3)).then_inc(a3h_ok, 1)

            def g_high():
                act.wait_ge(g_full, 1)
                cp(g_hl[:, 0], p_out[0][:]).then_inc(gh_ok, 1)

            def weights_out(kind, c, dst):
                n = use(kind, c)
                act.wait_ge(tr_full, n + 1)
                cp(dst[:, c], p_tr[n % 2][:]).then_inc(tr_act, 1)

            transposed_hi("x", 0, xt_of(0)[0])
            transposed_hi("x", 1, xt_of(0)[0])
            for i, q in enumerate(FIRST):
                act.wait_ge(w0_diag, i + 1)
                o = slice(q * P, (q + 1) * P)
                cp(w0_hi[:, :, o], stage_a[:, :, o]).then_inc(w0h_ok, 1)
            act.wait_ge(in_a0_first, 32)
            a0_high(0, 2)
            b0_high(0)
            transposed_hi("x", 2, xt_of(1)[0])
            transposed_hi("x", 3, xt_of(1)[0])
            xr_high(0)
            b0_high(1)
            act.wait_ge(in_a0, 16 * (NB - 2))
            a0_high(2, NB - 2)
            weights_out("w1", 0, w1_t)
            x1_high(0, 0)
            weights_out("w1", 1, w1_t)
            x1_high(0, 1)
            weights_out("w1", 2, w1_t)
            xr_high(1)
            weights_out("w1", 3, w1_t)
            act.wait_ge(const_ok, 6)
            m_high(0)
            x1_high(1, 0)
            weights_out("w3", 0, w3_hi)
            weights_out("w3", 1, w3_hi)
            x1_high(1, 1)
            m_high(1)
            act.wait_ge(tr_full, use("bw", 0) + 1)
            cp(bw_t[:], p_tr[use("bw", 0) % 2][:], scale=0.5).then_inc(tr_act, 1)
            weights_out("w3", 2, w3_hi)
            weights_out("w3", 3, w3_hi)
            a2_high()
            b2_high()
            m_high(2)
            transposed_hi("x2", 0, x2_of(0)[0])
            transposed_hi("x", 4, xt_hi)
            a3_high()
            g_high()
            transposed_hi("x", 5, xt_hi)
            b0_high(2)
            rows = slice(32, 64)
            cp(up[rows, 0, 0], bw_t[rows, :]).then_inc(upc_h, 1)
            transposed_hi("x2", 1, x2_of(0)[0])
            for p in range(1, PAIRS - 1):
                xr_high(p + 1)
                m_high(2 * p + 1)
                if p == 1:
                    act.wait_ge(upc_l, 1)
                    for h, s in ((0, 1), (1, 0), (1, 1)):
                        act.dma_start(f32(up[h * HALF + 32:h * HALF + 64, s]), f32(up[rows, 0])).then_inc(in_upc, 16)
                uw_high(2 * p - 2)
                uw_high(2 * p - 1)
                m_high(2 * p + 2)
                x1_high(p + 1, 0)
                x1_high(p + 1, 1)
                if p == PAIRS - 2:
                    m_high(NB - 1)
                out_copy(2 * p - 2)
                if p + 2 < PAIRS:
                    transposed_hi("x", 2 * p + 4, xt_hi)
                    transposed_hi("x", 2 * p + 5, xt_hi)
                out_copy(2 * p - 1)
                transposed_hi("x2", 2 * p, x2_of(p)[0])
                transposed_hi("x2", 2 * p + 1, x2_of(p)[0])
                if p + 2 < PAIRS:
                    b0_high(p + 2)
            uw_high(NB - 4)
            uw_high(NB - 3)
            out_copy(NB - 4)
            transposed_hi("x2", NB - 2, x2_of(PAIRS - 1)[0])
            transposed_hi("x2", NB - 1, x2_of(PAIRS - 1)[0])
            out_copy(NB - 3)
            uw_high(NB - 2)
            uw_high(NB - 1)
            out_copy(NB - 2)
            act.wait_ge(stored[(NB - 1) % C], 16 * ((NB - 1) // C))
            for h, bank in enumerate((p_out[1], p_l1)):
                act.wait_ge(out_full, NB + h)
                cols = slice(h * D // 2, (h + 1) * D // 2)
                cp(stage_b[:, (NB - 1) % C, cols], bank[:, cols]).then_inc(out_ok, 1)

        @block.vector
        def _(dve):
            def lo(o, full, hi):
                return nc.vector.tensor_tensor(o, full, f32(hi), ALU.subtract)

            def transposed_lo(kind, b, hi, dst):
                n = use(kind, b)
                dve.wait_ge(tr_act, n + 1)
                cols = slice((b % 2) * P, (b % 2 + 1) * P)
                lo(dst[:, :, cols], p_tr[n % 2][:].rearrange("p (c t) -> p c t", c=C), hi[:, :, cols]).then_inc(tr_dve, 1)

            def x1_low(p, h):
                dve.wait_ge(x1h_ok, 2 * p + h + 1)
                at = slice(2 * h, 2 * h + 2)
                hi, low = x1_of(p)
                lo(low[:, at], p_l0[:, at], hi[:, at]).then_inc(x1l_ok, 1)

            def b0_low(p):
                dve.wait_ge(b0h_ok, p + 1)
                lo(b0_lo[:, p % 2], b0_of(p), b0_hi[:, p % 2]).then_inc(b0l_ok, 1)

            def xr_stack(p):
                dve.wait_ge(xr_ok, p + 1)
                for s in range(2):
                    rows, cols = slice(s * HALF, (s + 1) * HALF), slice(s * P, (s + 1) * P)
                    nc.vector.scalar_tensor_tensor(xr_st[rows, cols], f32(xr[rows, cols]), lo_row[rows, 0:1],
                                                   p_dn[rows, 0, cols], ALU.mult, ALU.add).then_inc(xrst_ok, 1)

            def mix_weights(b, halves=(0, 1)):
                dve.wait_ge(in_mask[b % 2], 16 * (b // 2 + 1))
                for h in halves:
                    if b == 0:
                        dve.wait_ge(tr_act, use("w1", 2 * h + 1) + 1)
                    at = slice(2 * h, 2 * h + 2)
                    nc.vector.scalar_tensor_tensor(mix[:, b % 2, at], mix[:, b % 2, at].bitcast(I32), c_two[:, b:b + 1],
                                                   w1_t[:, at], ALU.mult, ALU.add).then_inc(mix_ok, 1)

            def m_low(b, halves=(0, 1)):
                for h in halves:
                    dve.wait_ge(mh_ok, 2 * b + h + 1)
                    at = slice(2 * h, 2 * h + 2)
                    nc.vector.scalar_tensor_tensor(m_lo[:, b % 2, at], mix[:, b % 2, at], c_neg[:, b:b + 1],
                                                   f32(m_hi[:, b % 2, at]), ALU.add, ALU.subtract).then_inc(ml_ok, 1)

            def x2_bias(b):
                dve.wait_ge(l1_full, b + 1)
                nc.vector.tensor_tensor(x2_nat[:, b % 2], p_l1[:], bias_bc[:], ALU.add).then_inc(x2_ok, 1)

            def uw_low(b):
                s = b % 2
                dve.wait_ge(uwh_ok, b + 1)
                rows, other = slice(s * HALF, (s + 1) * HALF), slice((1 - s) * HALF, (2 - s) * HALF)
                lo(uw_st[other, s, :], p_dn[rows, 1, s * P:(s + 1) * P], uw_st[rows, s, :]).then_inc(uwl_ok, 1)

            def a2_low():
                dve.wait_ge(a2h_ok, 1)
                lo(a2_lo[:], a2, a2_hi[:]).then_inc(a2l_ok, 1)

            def b2_low():
                n = use("b2", 0)
                dve.wait_ge(tr_act, n + 1)
                lo(d_lo[:, :, :, 0:R2].rearrange("p c b r -> p (c b) r"),
                   p_tr[n % 2][:].rearrange("p (c b r) -> p (c b) r", c=C, r=R2),
                   d_hi[:, :, :, 0:R2].rearrange("p c b r -> p (c b) r")).then_inc(tr_dve, 1)

            def a3_low():
                dve.wait_ge(a3h_ok, 1)
                lo(d_lo[:, :, :, 32:64].rearrange("p c b r -> p (c b) r"),
                   a3[:].rearrange("p c (b r) -> p (c b) r", r=R3),
                   d_hi[:, :, :, 32:64].rearrange("p c b r -> p (c b) r")).then_inc(a3l_ok, 1)

            def own_blocks():
                dve.wait_ge(ht_full, 1)
                dve.wait_ge(fill_ok, 2)
                for g in range(2):
                    own = slice(g * HALF, (g + 1) * HALF)
                    nc.vector.tensor_tensor(h_t[:, g, own], p_out[1][:, own], same[:], ALU.mult).then_inc(ht_ok, 1)

            def g_low():
                dve.wait_ge(gh_ok, 1)
                lo(g_hl[:, 1], p_out[0][:], g_hl[:, 0]).then_inc(gl_ok, 1)

            def w3_low(c):
                n = use("w3", c)
                dve.wait_ge(tr_act, n + 1)
                lo(w3_lo[:, c], p_tr[n % 2][:], w3_hi[:, c]).then_inc(tr_dve, 1)

            def w0_identity(q):
                dve.wait_ge(in_w0[q], 16)
                at = stage_a[:, q, q * P:(q + 1) * P]
                nc.vector.tensor_tensor(at, at, ident, ALU.add).then_inc(w0_diag, 1)

            def w1_identity():
                dve.wait_ge(in_w1, 16)
                at = bass.AP(stage_b, 0, [[C * D, P], [D + P, C], [1, P]])
                eye = bass.AP(ident_r, 0, [[P, P], [0, C], [1, P]])
                nc.vector.tensor_tensor(at, at, eye, ALU.add).then_inc(w1_diag, 1)

            def w0_low(i):
                dve.wait_ge(w0h_ok, i + 1)
                o = slice(FIRST[i] * P, (FIRST[i] + 1) * P)
                lo(w0_lo[:, :, o], stage_a[:, :, o], w0_hi[:, :, o]).then_inc(w0l_ok, 1)

            def a0_low(b, n, done):
                for rep in range(2):
                    dve.wait_ge(a0h_ok, done + rep + 1)
                    lo(a0_st[:, :, b:b + n, rep, 1, :], a0[:, :, b:b + n, :],
                       a0_st[:, :, b:b + n, rep, 0, :]).then_inc(a0l_ok, 1)

            dve.wait_ge(ident_ok, 1)
            transposed_lo("x", 0, *xt_of(0))
            w0_identity(FIRST[0])
            transposed_lo("x", 1, *xt_of(0))
            w0_low(0)
            w0_identity(FIRST[1])
            w0_identity(FIRST[2])
            w0_low(1)
            w0_identity(FIRST[3])
            w0_low(2)
            a0_low(0, 2, 0)
            w0_low(3)
            b0_low(0)
            dve.wait_ge(const_ok, 4)
            transposed_lo("x", 2, *xt_of(1))
            transposed_lo("x", 3, *xt_of(1))
            xr_stack(0)
            w1_identity()
            b0_low(1)
            a0_low(2, NB - 2, 2)
            x1_low(0, 0)
            dve.wait_ge(const_ok, 6)
            mix_weights(0, [0])
            x1_low(0, 1)
            xr_stack(1)
            mix_weights(0, [1])
            m_low(0)
            mix_weights(1, [0])
            x1_low(1, 0)
            w3_low(0)
            w3_low(1)
            mix_weights(1, [1])
            x1_low(1, 1)
            m_low(1)
            w3_low(2)
            dve.wait_ge(tr_full, use("bw", 0) + 1)
            dve.wait_ge(in_bias, 16)
            x2_bias(0)
            w3_low(3)
            a2_low()
            mix_weights(2, [0])
            b2_low()
            own_blocks()
            mix_weights(2, [1])
            x2_bias(1)
            m_low(2)
            transposed_lo("x2", 0, *x2_of(0))
            transposed_lo("x", 4, xt_hi, xt_lo)
            a3_low()
            transposed_lo("x", 5, xt_hi, xt_lo)
            b0_low(2)
            g_low()
            transposed_lo("x2", 1, *x2_of(0))
            xr_stack(2)
            x2_bias(2)
            dve.wait_ge(upc_h, 1)
            lo(up[32:64, 0, 1], bw_t[32:64, :], up[32:64, 0, 0]).then_inc(upc_l, 1)
            mix_weights(3)
            for p in range(1, PAIRS - 1):
                if p >= 2:
                    x2_bias(2 * p)
                    xr_stack(p + 1)
                    mix_weights(2 * p + 1)
                m_low(2 * p + 1)
                uw_low(2 * p - 2)
                uw_low(2 * p - 1)
                mix_weights(2 * p + 2)
                m_low(2 * p + 2)
                x1_low(p + 1, 0)
                x1_low(p + 1, 1)
                x2_bias(2 * p + 1)
                if p == PAIRS - 2:
                    mix_weights(NB - 1)
                    m_low(NB - 1)
                if p + 2 < PAIRS:
                    transposed_lo("x", 2 * p + 4, xt_hi, xt_lo)
                    transposed_lo("x", 2 * p + 5, xt_hi, xt_lo)
                transposed_lo("x2", 2 * p, *x2_of(p))
                transposed_lo("x2", 2 * p + 1, *x2_of(p))
                if p + 2 < PAIRS:
                    b0_low(p + 2)
            x2_bias(NB - 2)
            uw_low(NB - 4)
            uw_low(NB - 3)
            x2_bias(NB - 1)
            transposed_lo("x2", NB - 2, *x2_of(PAIRS - 1))
            transposed_lo("x2", NB - 1, *x2_of(PAIRS - 1))
            uw_low(NB - 2)
            uw_low(NB - 1)

        @block.tensor
        def _(pe):
            mm = nc.tensor.matmul

            def bank_free(n):
                if n >= 2:
                    pe.wait_ge(tr_act, n - 1)
                    if dve_reads(n - 2):
                        pe.wait_ge(tr_dve, dve_reads(n - 2))

            def transpose4(kind, i, blocks):
                n = use(kind, i)
                bank_free(n)
                for c in range(C):
                    t = nc.tensor.transpose(p_tr[n % 2][:, c * P:(c + 1) * P], blocks(c), ident)
                t.then_inc(tr_full, 1)

            def transpose_w1(i):
                transpose4("w1", i, lambda q: stage_b[:, q, i * P:(i + 1) * P])

            def transpose_w3(i):
                n = use("w3", i)
                bank_free(n)
                for c in range(C):
                    o, w = p_tr[n % 2][:, c * P:(c + 1) * P], stage_a[:, c, i * P:(i + 1) * P]
                    if c == i:
                        mm(o, w, ident, start=True, stop=False)
                        t = mm(o, ident_r[:], ident_r[:], start=False, stop=True)
                    else:
                        t = nc.tensor.transpose(o, w, ident)
                t.then_inc(tr_full, 1)

            def transpose_x(b):
                if b == 0:
                    pe.wait_ge(in_x_first, 16)
                else:
                    pe.wait_ge(in_x[b // 2 % 2], 16 * (b // 4 + 1))
                transpose4("x", b, lambda c: x_nat[:, b // 2 % 2, b % 2, c * P:(c + 1) * P])

            def transpose_x2(b):
                pe.wait_ge(x2_ok, b + 1)
                transpose4("x2", b, lambda c: x2_nat[:, b % 2, c * P:(c + 1) * P])

            def down0(p):
                pe.wait_ge(tr_act, use("x", 2 * p + 1) + 1)
                pe.wait_ge(tr_dve, dve_reads(use("x", 2 * p + 1)))
                pe.wait_ge(a0l_ok, 2 if p == 0 else 4)
                if p >= 1:
                    pe.wait_ge(xrst_ok, 2 * p)
                if p >= 3:
                    pe.wait_ge(uwl_ok, 2 * (p - 2))
                for c in range(C):
                    w = a0_st[:, c, 2 * p:2 * p + 2].rearrange("p b e h r -> p (b e h r)")
                    mm(p_dn[:, 0], w, xt_of(p)[0][:, c], start=(c == 0), stop=False)
                    t = mm(p_dn[:, 0], w, xt_of(p)[1][:, c], start=False, stop=(c == C - 1))
                t.then_inc(dn0_full, 1)

            def layer0_main(p, q):
                if p >= 1 and q % 2 == 0:
                    pe.wait_ge(x1l_ok, 2 * (p - 1) + q // 2 + 1)
                x_hi, x_lo = xt_of(p)
                o = slice(q * P, (q + 1) * P)
                passes = ((w0_hi, x_hi), (w0_hi, x_lo), (w0_lo, x_hi))
                for i, (w, x) in enumerate(passes):
                    if p == 0 and q == 0:
                        if i == 0:
                            pe.wait_ge(w0h_ok, 1)
                            pe.wait_ge(tr_act, use("x", 1) + 1)
                        elif i == 1:
                            pe.wait_ge(tr_dve, dve_reads(use("x", 1)))
                        else:
                            pe.wait_ge(w0l_ok, 1)
                    elif p == 0 and i == 0:
                        pe.wait_ge(w0l_ok, FIRST.index(q) + 1)
                    for c in range(C):
                        mm(p_l0[:, q], w[:, c, o], x[:, c], start=(i == 0 and c == 0 and q % 2 == 0), stop=False)

            def layer0_side(p, q):
                if q == 0:
                    pe.wait_ge(xrst_ok, 2 * p + 2)
                    pe.wait_ge(b0l_ok, p + 1)
                o = slice(q * P, (q + 1) * P)
                mm(p_l0[:, q], b0_hi[:, p % 2, o], xr_st[:], start=False, stop=False)
                t = mm(p_l0[:, q], b0_lo[:, p % 2, o], xr_st[:], start=False, stop=(q % 2 == 1))
                if q % 2:
                    t.then_inc(l0_full, 1)

            def layer1(b):
                pe.wait_ge(x1l_ok, 2 * (b // 2) + 2)
                if b >= 1:
                    pe.wait_ge(x2_ok, b)
                tok = slice((b % 2) * P, (b % 2 + 1) * P)
                x1_hi, x1_lo = x1_of(b // 2)
                for c in range(C):
                    if c % 2 == 0:
                        pe.wait_ge(ml_ok, 2 * b + c // 2 + 1)
                    mm(p_l1[:], x1_hi[:, c, tok], m_hi[:, b % 2, c], start=(c == 0), stop=False)
                    mm(p_l1[:], x1_hi[:, c, tok], m_lo[:, b % 2, c], start=False, stop=False)
                    t = mm(p_l1[:], x1_lo[:, c, tok], m_hi[:, b % 2, c], start=False, stop=(c == C - 1))
                t.then_inc(l1_full, 1)

            def down2(p):
                pe.wait_ge(tr_act, use("x2", 2 * p + 1) + 1)
                pe.wait_ge(tr_dve, dve_reads(use("x2", 2 * p + 1)))
                if p == 0:
                    pe.wait_ge(tr_dve, dve_reads(use("b2", 0)))
                    pe.wait_ge(a3l_ok, 1)
                else:
                    pe.wait_ge(uwl_ok, 2 * p)
                pe.wait_ge(xrst_ok, 2 * min(p + 3, PAIRS))
                x2_hi, x2_lo = x2_of(p)
                for c in range(C):
                    wh = d_hi[:, c, 2 * p:2 * p + 2].rearrange("p b r -> p (b r)")
                    wl = d_lo[:, c, 2 * p:2 * p + 2].rearrange("p b r -> p (b r)")
                    mm(p_dn[:, 1], wh, x2_hi[:, c], start=(c == 0), stop=False)
                    mm(p_dn[:, 1], wh, x2_lo[:, c], start=False, stop=False)
                    t = mm(p_dn[:, 1], wl, x2_hi[:, c], start=False, stop=(c == C - 1))
                t.then_inc(dn2_full, 1)

            def layer23_main(b, bank, cols=slice(0, D)):
                s = b % 2
                tok = slice(s * P, (s + 1) * P)
                x2_hi, x2_lo = x2_of(b // 2)
                if b == 0:
                    pe.wait_ge(tr_dve, dve_reads(use("w3", C - 1)))
                    pe.wait_ge(gl_ok, 1)
                if b >= 2:
                    pe.wait_ge(out_ok, b - 1)
                for c in range(C):
                    mm(bank[:, cols], x2_hi[:, c, tok], w3_hi[:, c, cols], start=(c == 0), stop=False)
                    mm(bank[:, cols], x2_hi[:, c, tok], w3_lo[:, c, cols], start=False, stop=False)
                    mm(bank[:, cols], x2_lo[:, c, tok], w3_hi[:, c, cols], start=False, stop=False)

            def layer23_side(b, bank, cols=slice(0, D)):
                s = b % 2
                pe.wait_ge(uwl_ok, b + 1)
                pe.wait_ge(in_up[s], 32 * (b // 2 + 1))
                if b < 2:
                    pe.wait_ge(in_upc, 48)
                mm(bank[:, cols], uw_st[:, s], up[:, s, 0, cols], start=False, stop=False)
                mm(bank[:, cols], uw_st[:, s], up[:, s, 1, cols], start=False, stop=True).then_inc(out_full, 1)

            def layer23(b):
                layer23_main(b, p_out[b % 2])
                layer23_side(b, p_out[b % 2])

            def adapters():
                pe.wait_ge(in_a2, 16 * NB)
                pe.wait_ge(in_a3, 16 * NB)
                for g in range(2):
                    for k in range(C):
                        t = mm(p_out[1][:, g * HALF:(g + 1) * HALF], a3[:, k, g * P:(g + 1) * P],
                               a2[:, k, g * HALF:(g + 1) * HALF],
                               start=(k == 0), stop=(k == C - 1))
                t.then_inc(ht_full, 1)
                pe.wait_ge(in_b2, 16 * NB)
                transpose4("b2", 0, lambda c: b2[:, c * P:(c + 1) * P])

            def up_projection():
                pe.wait_ge(a2l_ok, 1)
                pe.wait_ge(tr_dve, dve_reads(use("w3", C - 1)))
                for k in range(C):
                    mm(p_out[0][:], a2_hi[:, k], w3_hi[:, k], start=(k == 0), stop=False)
                    mm(p_out[0][:], a2_hi[:, k], w3_lo[:, k], start=False, stop=False)
                    mm(p_out[0][:], a2_lo[:, k], w3_hi[:, k], start=False, stop=False)
                pe.wait_ge(ht_ok, 2)
                pe.wait_ge(tr_act, use("bw", 0) + 1)
                for g in range(2):
                    t = mm(p_out[0][:], h_t[:, g], bw_t[:], start=False, stop=(g == 1))
                t.then_inc(g_full, 1)

            def warm_up(n):
                for _ in range(n):
                    mm(p_out[1][:, 0:P], ident, ident, start=True, stop=True)

            pe.wait_ge(ident_ok, 1)
            warm_up(4)
            transpose_x(0)
            transpose_x(1)
            warm_up(6)
            layer0_main(0, 0)
            transpose_x(2)
            transpose_x(3)
            layer0_main(0, 2)
            layer0_main(0, 1)
            down0(0)
            layer0_main(0, 3)
            for q in range(C):
                layer0_side(0, q)
            pe.wait_ge(w1_diag, 1)
            for c in range(C):
                if c == 2:
                    down0(1)
                transpose_w1(c)
            layer0_main(1, 0)
            layer0_main(1, 2)
            layer0_side(1, 0)
            layer0_main(1, 1)
            layer0_side(1, 1)
            pe.wait_ge(in_w3, 16)
            transpose_w3(0)
            layer0_side(1, 2)
            transpose_w3(1)
            layer0_main(1, 3)
            layer0_side(1, 3)
            layer1(0)
            pe.wait_ge(bw_ok, 4)
            transpose4("bw", 0, lambda c: bw_rep[:, c, :])
            transpose_w3(2)
            transpose_w3(3)
            adapters()
            layer1(1)
            transpose_x2(0)
            transpose_x(4)
            up_projection()
            transpose_x(5)
            for p in range(1, PAIRS - 1):
                layer1(2 * p)
                if p == 1:
                    transpose_x2(1)
                down0(p + 1)
                layer0_main(p + 1, 0)
                down2(p - 1)
                layer0_side(p + 1, 0)
                for q in range(1, C):
                    layer0_main(p + 1, q)
                    layer0_side(p + 1, q)
                layer1(2 * p + 1)
                layer23(2 * p - 2)
                if p + 2 < PAIRS:
                    transpose_x(2 * p + 4)
                    transpose_x(2 * p + 5)
                layer23(2 * p - 1)
                transpose_x2(2 * p)
                transpose_x2(2 * p + 1)
            layer1(NB - 2)
            down2(PAIRS - 2)
            layer1(NB - 1)
            layer23(NB - 4)
            transpose_x2(NB - 2)
            transpose_x2(NB - 1)
            layer23(NB - 3)
            down2(PAIRS - 1)
            layer23(NB - 2)
            for h, bank in enumerate((p_out[1], p_l1)):
                cols = slice(h * D // 2, (h + 1) * D // 2)
                layer23_main(NB - 1, bank, cols)
                layer23_side(NB - 1, bank, cols)


_INS = ["x", "itok_B_0_15", "condB_coeff", "itok_B_3_7", "itok_B_0_2", "mask_Bx4096x4096_ik1",
        "L0_cond_W", "L0_cond_lora_A", "L0_cond_lora_B", "L1_cond_W", "L1_cond_b",
        "L2_cond_A", "L2_cond_B", "L3_cond_W", "L3_cond_lora_A", "L3_cond_lora_B_w"]


def kernel(**inputs):
    import numpy as _np
    import concourse.bacc as _bacc
    from concourse import mybir as _mybir
    from concourse.bass_utils import run_bass_kernel_spmd as _run

    nc = _bacc.Bacc("TRN2", target_bir_lowering=False, num_devices=1)
    arrays, args = {}, []
    for name in _INS:
        a = _np.ascontiguousarray(inputs[name])
        arrays[f"in_{name}_dram"] = a
        args.append(nc.dram_tensor(f"in_{name}_dram", a.shape, _mybir.dt.from_np(a.dtype), kind="ExternalInput").ap())
    shape = inputs["x"].shape
    args.append(nc.dram_tensor("out_0_dram", shape, _mybir.dt.float32, kind="ExternalOutput").ap())
    build(nc, *args)
    r = _run(nc, [arrays], core_ids=[0])
    return r.results[0]["out_0_dram"]
```
